# Optimizing a Trainium2 kernel written in Bass

```python
import numpy as np
import jax
import jax.numpy as jnp

def _softmax(x, axis=-1):
    return jax.nn.softmax(x, axis=axis)

def _gelu(x):
    return jax.nn.gelu(x, approximate=True)

def _silu(x):
    return jax.nn.silu(x)

def _sigmoid(x):
    return jax.nn.sigmoid(x)

def _layernorm(x, axis=-1, eps=1e-05):
    m = jnp.mean(x, axis=axis, keepdims=True)
    v = jnp.var(x, axis=axis, keepdims=True)
    return (x - m) / jnp.sqrt(v + eps)

def _scatter_add(tgt, idx, src, axis=0):
    return tgt.at[idx].add(src)

def _segment_sum(src, seg, n):
    return jax.ops.segment_sum(src, seg, n)
kernel_name = 'mk_sandwich_d1_jaxref_r2_0fa37c'

def setup_inputs(seed: int=0):
    np.random.seed(seed)
    _w = jnp.asarray

    def _L0_attn_setup():
        import jax, jax.numpy as jnp
        import numpy as np
        from jax import lax
        D = 512
        K = 3
        LN_EPS = 1e-05

        def _dwconv(v, conv_w, conv_b):
            vt = jnp.transpose(v, (0, 2, 1))
            out = lax.conv_general_dilated(vt, conv_w, window_strides=(1,), padding=[(K // 2, K // 2)], dimension_numbers=('NCH', 'OIH', 'NCH'), feature_group_count=D)
            out = out + conv_b[None, :, None]
            return jnp.transpose(out, (0, 2, 1))
        key = jax.random.key(seed)
        ks = jax.random.split(key, 8)
        B, T = (8, 2048)
        x = jax.random.normal(ks[0], (B, T, D), dtype=jnp.float32)
        s = 1.0 / np.sqrt(D)
        in_proj_w = jax.random.uniform(ks[1], (D, 2 * D), jnp.float32, -s, s)
        in_proj_b = jax.random.uniform(ks[2], (2 * D,), jnp.float32, -s, s)
        conv_w = jax.random.uniform(ks[3], (D, 1, K), jnp.float32, -1.0 / np.sqrt(K), 1.0 / np.sqrt(K))
        conv_b = jax.random.uniform(ks[4], (D,), jnp.float32, -1.0 / np.sqrt(K), 1.0 / np.sqrt(K))
        logit_a = jnp.zeros((D,), jnp.float32)
        ssm_b = jnp.full((D,), 0.1, jnp.float32)
        ssm_c = jnp.ones((D,), jnp.float32)
        ssm_d = jnp.zeros((D,), jnp.float32)
        out_proj_w = jax.random.uniform(ks[5], (D, D), jnp.float32, -s, s)
        out_proj_b = jax.random.uniform(ks[6], (D,), jnp.float32, -s, s)
        ln_w = jnp.ones((D,), jnp.float32)
        ln_b = jnp.zeros((D,), jnp.float32)
        return {'x': x, 'in_proj_w': in_proj_w, 'in_proj_b': in_proj_b, 'conv_w': conv_w, 'conv_b': conv_b, 'logit_a': logit_a, 'ssm_b': ssm_b, 'ssm_c': ssm_c, 'ssm_d': ssm_d, 'out_proj_w': out_proj_w, 'out_proj_b': out_proj_b, 'ln_w': ln_w, 'ln_b': ln_b}
    _L0_attn_in = _L0_attn_setup()

    def _L0_ffn_setup():
        import jax, jax.numpy as jnp
        import numpy as np
        EMB = 512
        FF = 4 * EMB

        def _ternary(w):
            scale = jnp.maximum(jnp.mean(jnp.abs(w)), 1e-08)
            w_t = jnp.clip(jnp.round(w / scale), -1.0, 1.0)
            return w + jax.lax.stop_gradient(w_t - w)
        key = jax.random.key(seed)
        kx, k1, k2, kb1, kb2 = jax.random.split(key, 5)
        x = jax.random.normal(kx, (4, 1024, EMB), dtype=jnp.float32)
        lim1 = 1.0 / np.sqrt(EMB)
        lim2 = 1.0 / np.sqrt(FF)
        W1 = jax.random.uniform(k1, (FF, EMB), jnp.float32, -lim1, lim1)
        b1 = jax.random.uniform(kb1, (FF,), jnp.float32, -lim1, lim1)
        W2 = jax.random.uniform(k2, (EMB, FF), jnp.float32, -lim2, lim2)
        b2 = jax.random.uniform(kb2, (EMB,), jnp.float32, -lim2, lim2)
        return {'x': x, 'W1': W1, 'b1': b1, 'W2': W2, 'b2': b2}
    _L0_ffn_in = _L0_ffn_setup()
    _d = {'L0_attn_x': _L0_attn_in['x'], 'L0_attn_in_proj_w': _L0_attn_in['in_proj_w'], 'L0_attn_in_proj_b': _L0_attn_in['in_proj_b'], 'L0_attn_conv_w': _L0_attn_in['conv_w'], 'L0_attn_conv_b': _L0_attn_in['conv_b'], 'L0_attn_logit_a': _L0_attn_in['logit_a'], 'L0_attn_ssm_b': _L0_attn_in['ssm_b'], 'L0_attn_ssm_c': _L0_attn_in['ssm_c'], 'L0_attn_ssm_d': _L0_attn_in['ssm_d'], 'L0_attn_out_proj_w': _L0_attn_in['out_proj_w'], 'L0_attn_out_proj_b': _L0_attn_in['out_proj_b'], 'L0_attn_ln_w': _L0_attn_in['ln_w'], 'L0_attn_ln_b': _L0_attn_in['ln_b'], 'L0_ffn_W1': _L0_ffn_in['W1'], 'L0_ffn_b1': _L0_ffn_in['b1'], 'L0_ffn_W2': _L0_ffn_in['W2'], 'L0_ffn_b2': _L0_ffn_in['b2']}
    _x0 = _d['L0_attn_x']
    _d['L0_attn_x'] = jax.random.normal(jax.random.fold_in(jax.random.key(seed), 1), (1, 8192, 512), dtype=_x0.dtype)
    del _x0
    return _d

def reference(L0_attn_x, L0_attn_in_proj_w, L0_attn_in_proj_b, L0_attn_conv_w, L0_attn_conv_b, L0_attn_logit_a, L0_attn_ssm_b, L0_attn_ssm_c, L0_attn_ssm_d, L0_attn_out_proj_w, L0_attn_out_proj_b, L0_attn_ln_w, L0_attn_ln_b, L0_ffn_W1, L0_ffn_b1, L0_ffn_W2, L0_ffn_b2):

    def _L0_attn_ref(x, in_proj_w, in_proj_b, conv_w, conv_b, logit_a, ssm_b, ssm_c, ssm_d, out_proj_w, out_proj_b, ln_w, ln_b):
        import jax, jax.numpy as jnp
        import numpy as np
        from jax import lax
        D = 512
        K = 3
        LN_EPS = 1e-05

        def _dwconv(v, conv_w, conv_b):
            vt = jnp.transpose(v, (0, 2, 1))
            out = lax.conv_general_dilated(vt, conv_w, window_strides=(1,), padding=[(K // 2, K // 2)], dimension_numbers=('NCH', 'OIH', 'NCH'), feature_group_count=D)
            out = out + conv_b[None, :, None]
            return jnp.transpose(out, (0, 2, 1))
        B, T, _ = x.shape
        residual = x
        uv = x @ in_proj_w + in_proj_b
        u, v = (uv[..., :D], uv[..., D:])
        v = jax.nn.silu(v)
        v_local = _dwconv(v, conv_w, conv_b)
        a = jax.nn.sigmoid(logit_a).astype(v_local.dtype)

        def step(h, vt):
            h = a * h + ssm_b * vt
            return (h, ssm_c * h + ssm_d * vt)
        h0 = jnp.zeros((B, D), v_local.dtype)
        _, y_seq = lax.scan(step, h0, jnp.transpose(v_local, (1, 0, 2)))
        y_seq = jnp.transpose(y_seq, (1, 0, 2))
        out = u * jax.nn.silu(y_seq)
        out = out @ out_proj_w + out_proj_b
        h = out + residual
        mu = jnp.mean(h, axis=-1, keepdims=True)
        var = jnp.mean(jnp.square(h - mu), axis=-1, keepdims=True)
        return (h - mu) * lax.rsqrt(var + LN_EPS) * ln_w + ln_b

    def _L0_ffn_ref(x, W1, b1, W2, b2):
        import jax, jax.numpy as jnp
        import numpy as np
        EMB = 512
        FF = 4 * EMB

        def _ternary(w):
            scale = jnp.maximum(jnp.mean(jnp.abs(w)), 1e-08)
            w_t = jnp.clip(jnp.round(w / scale), -1.0, 1.0)
            return w + jax.lax.stop_gradient(w_t - w)
        h = jnp.einsum('bsd,fd->bsf', x, _ternary(W1)) + b1
        h = jax.nn.gelu(h, approximate=False)
        out = jnp.einsum('bsf,df->bsd', h, _ternary(W2)) + b2
        return out
    x = L0_attn_x
    x = x + _layernorm(_L0_attn_ref(_layernorm(x, axis=-1), L0_attn_in_proj_w, L0_attn_in_proj_b, L0_attn_conv_w, L0_attn_conv_b, L0_attn_logit_a, L0_attn_ssm_b, L0_attn_ssm_c, L0_attn_ssm_d, L0_attn_out_proj_w, L0_attn_out_proj_b, L0_attn_ln_w, L0_attn_ln_b), axis=-1)
    x = x + _layernorm(_L0_ffn_ref(_layernorm(x, axis=-1), L0_ffn_W1, L0_ffn_b1, L0_ffn_W2, L0_ffn_b2), axis=-1)
    return x

_drawn_inputs = setup_inputs


def setup_inputs(seed=0):
    import zlib

    import numpy as np

    out = dict(_drawn_inputs(seed))
    spreads = {'L0_attn_logit_a': (0.0, 0.8),
     'L0_attn_ssm_b': (0.10000000149011612, 0.6),
     'L0_attn_ssm_c': (1.0, 0.6),
     'L0_attn_ssm_d': (0.0, 0.8),
     'L0_attn_ln_w': (1.0, 0.2),
     'L0_attn_ln_b': (0.0, 0.1)}
    factors = {'L0_attn_in_proj_w': 8.0,
     'L0_attn_in_proj_b': 8.0,
     'L0_attn_conv_w': 8.0,
     'L0_attn_conv_b': 8.0,
     'L0_attn_out_proj_w': 8.0,
     'L0_attn_out_proj_b': 35.704,
     'L0_ffn_b1': 64.0,
     'L0_ffn_b2': 64.0}
    for name, (base, spread) in spreads.items():
        noise = np.random.default_rng([zlib.crc32(name.encode()), seed]).standard_normal(out[name].shape)
        drawn = base * np.exp(spread * noise) if base else spread * noise
        out[name] = jnp.asarray(drawn.astype(out[name].dtype))
    for name, factor in factors.items():
        out[name] = (out[name] * factor).astype(out[name].dtype)
    return out
```

```python
from contextlib import ExitStack

import concourse.bass as bass
from concourse import mybir

P = 128
D = 512
TT = 512
NB = TT // P
KC = D // P
LAG = 2
X_SLOTS = 4
G_SLOTS = 3
H_SLOTS = 4
EPS = 1e-5
ACT_SCALE = 2048.0

F32 = mybir.dt.float32
F32R = mybir.dt.float32r
F16 = mybir.dt.float16
U32 = mybir.dt.uint32
ALU = mybir.AluOpType
ACT = mybir.ActivationFunctionType
AX = mybir.AxisListType

BIN, CW, CB, LA, SB, SC, SD, B1 = 0, 8, 20, 24, 28, 32, 36, 40
NPAR = 56


AT_F_ADD, AT_F_STATS, AT_F_AGGR, AT_F_NORM = 0.0, 0.8, 1.6, 2.6
AT_PAIR = (2.0, 4.1)
AT_LN1, AT_RES = 6.2, 6.5
AT_NORMS = 8.1


def run(items):
    for _, work in sorted(items, key=lambda item: item[0]):
        work()


def spread(at, step, works):
    return [(at + step * i, w) for i, w in enumerate(works)]


def build(nc, x, w_in, w_out, w1t, w2t, params, rows, out):
    T = x.shape[0]
    NT = T // TT
    FF = w1t.shape[1]
    FC = FF // P
    HALF = FC // 2
    STEPS = range(-1, NT + 2)

    x_d = x.rearrange("(t j p) d -> t p j d", p=P, j=NB)
    out_d = out.rearrange("(t j p) d -> t j p d", p=P, j=NB)
    w_in_d = w_in.rearrange("(k p) n -> p k n", p=P)
    w_out_d = w_out.rearrange("(k p) n -> p k n", p=P)
    w1_d = w1t.rearrange("(k p) (q n) -> k q p n", p=P, n=512)
    w2_d = w2t.rearrange("(c p) n -> c p n", p=P)
    NQ = FF // 512
    chunks = [w1_d[i // NQ, i % NQ] for i in range(KC * NQ)] + [w2_d[c] for c in range(FC)]
    NCH = len(chunks)

    with ExitStack() as ctx:
        def sb(name, shape, dt=F32):
            return ctx.enter_context(nc.sbuf_tensor(name, shape, dt))

        def sem(name):
            return ctx.enter_context(nc.semaphore(name))

        win_hi = sb("win_hi", [P, KC, 2 * D], F16)
        win_lo = sb("win_lo", [P, KC, 2 * D], F16)
        wo_hi = sb("wo_hi", [P, KC, D], F32R)
        wo_lo = sb("wo_lo", [P, KC, D], F32R)
        w1 = sb("w1", [P, KC, FF], F16)
        w2 = sb("w2", [P, FC, D], F16)
        row = sb("row", [P, 4, D])
        ob_row, lnw_row, lnb_row, b2_row = (row[:, i, :] for i in range(4))
        ident = sb("ident", [P, P])
        par = sb("par", [P, NPAR])
        xs = sb("xs", [P, X_SLOTS, NB, D])
        xn = sb("xn", [P, 2, D])
        hb = sb("hb", [P, NB, D])
        x1T_hi = sb("x1T_hi", [P, 2, KC, TT], F16)
        x1T_lo = sb("x1T_lo", [P, 2, KC, TT], F16)
        x3T_hi = sb("x3T_hi", [P, KC, TT], F16)
        x3T_lo = sb("x3T_lo", [P, KC, TT], F16)
        vb = sb("vb", [P, 2 * KC * (TT + 2)])
        v = vb[:, :].rearrange("p (s k t) -> p s k t", s=2, k=KC)
        vl = sb("vl", [P, 2, TT])
        ss = sb("ss", [P, 2, TT])
        yb = sb("yb", [P, KC, TT])
        g_hi = sb("g_hi", [P, KC, TT], F32R)
        g_lo = sb("g_lo", [P, KC, TT], F32R)
        gg = sb("gg", [P, G_SLOTS, TT])
        h_hi = sb("h_hi", [P, H_SLOTS, TT], F16)
        h_lo = sb("h_lo", [P, H_SLOTS, TT], F16)
        bn = sb("bn", [P, 5, NB, 6])
        mv = sb("mv", [P, 5, NB, 2])
        ve = sb("ve", [P, 5, NB])
        rs1 = sb("rs1", [P, 4, NB])
        nm1 = sb("nm1", [P, 4, NB])
        rsc = sb("rsc", [P, 3, NB])
        c0 = sb("c0", [P, 4, NB])
        rs4 = sb("rs4", [P, NB])
        nm4 = sb("nm4", [P, NB])
        mhalf = sb("mhalf", [P, NB])
        carry = sb("carry", [P, KC])
        tmp4 = sb("tmp4", [P, 3, NB])
        ones = sb("ones", [P, P])
        wmax = sb("wmax", [P, 4])
        wrow = sb("wrow", [P, 4])
        sig = sb("sig", [P, 1])
        inv_sig = sb("inv_sig", [P, 1])
        bu_sig = sb("bu_sig", [P, KC])
        a_par = sb("a_par", [P, KC])
        cb_par = sb("cb_par", [P, KC])
        f_sc = sb("f_sc", [P, FC])
        f_inv = sb("f_inv", [P, FC])
        asum = sb("asum", [P, NCH])
        thr = sb("thr", [P, 4])
        thr_s = sb("thr_s", [P, 2])

        misc = [ctx.enter_context(nc.psum_tensor(f"misc{i}", [P, 512], F32)) for i in range(2)]
        f1b = [ctx.enter_context(nc.psum_tensor(f"f1b{i}", [P, 512], F32)) for i in range(2)]
        f2b = [ctx.enter_context(nc.psum_tensor(f"f2b{i}", [P, 512], F32)) for i in range(NB)]

        x_in = [sem(f"x_in{i}") for i in range(X_SLOTS)]
        par_in, win_in, wout_in, row_in = sem("par_in"), sem("win_in"), sem("wout_in"), sem("row_in")
        chunk_in = [sem(f"chunk_in{i}") for i in range(G_SLOTS)]
        out_st = [sem(f"out_st{i}") for i in range(NB)]
        const_ok, prep, pmx, pm1 = sem("const_ok"), sem("prep"), sem("pmx"), sem("pm1")
        win_h, win_l, wo_h, wo_l = sem("win_h"), sem("win_l"), sem("wo_h"), sem("wo_l")
        abs_ok, thr_ok, thr_mm, t_ok, w_ok, w2_ok = (
            sem("abs_ok"), sem("thr_ok"), sem("thr_mm"), sem("t_ok"), sem("w_ok"), sem("w2_ok"))
        a_ok, tanh_ok = sem("a_ok"), sem("tanh_ok")
        bn_ok = [sem(f"bn_ok{i}") for i in range(5)]
        mv_ok = [sem(f"mv_ok{i}") for i in range(5)]
        ve_ok, pool_ok = sem("ve_ok"), sem("pool_ok")
        rs_ok = [sem(f"rs_ok{i}") for i in range(5)]
        xn_ok, t1_mm, x1_hi, x1_lo, v_mm, v_ok = (
            sem("xn_ok"), sem("t1_mm"), sem("x1_hi"), sem("x1_lo"), sem("v_mm"), sem("v_ok"))
        left_ok, right_ok = sem("left_ok"), sem("right_ok")
        tap1, tap0, tap2, scan_ok, carry_ok, dv_ok, y_ok, sy_ok, u_mm, g_ok, ghi_ok, glo_ok = (
            sem("tap1"), sem("tap0"), sem("tap2"), sem("scan_ok"), sem("carry_ok"), sem("dv_ok"),
            sem("y_ok"), sem("sy_ok"), sem("u_mm"), sem("g_ok"), sem("ghi_ok"), sem("glo_ok"))
        res_ok, resb_ok, o_mm, h_ok, a1_ok, a2_ok, x1_ok, n3_ok, t3_mm, x3_hi, x3_lo = (
            sem("res_ok"), sem("resb_ok"), sem("o_mm"), sem("h_ok"), sem("a1_ok"), sem("a2_ok"),
            sem("x1_ok"), sem("n3_ok"), sem("t3_mm"), sem("x3_hi"), sem("x3_lo"))
        f1_mm, gelu_ok, hh_ok, hl_ok, f2_mm, f_ok, fn_ok, fin_ok = (
            sem("f1_mm"), sem("gelu_ok"), sem("hh_ok"), sem("hl_ok"), sem("f2_mm"), sem("f_ok"),
            sem("fn_ok"), sem("fin_ok"))

        def tiles(s):
            return [t if 0 <= t < NT else None for t in (s - 2, s - 1, s + 1, s - 3)]

        groups = []
        for s in STEPS:
            fa, c, n, _ = tiles(s)
            if c is not None:
                groups += [("u", c, b) for b in range(KC)]
            if n is not None:
                groups += [("t1", n, j) for j in range(NB)] + [("v", n, 0)]
            if c is not None:
                groups += [("o", c, j) for j in range(NB)]
            if n is not None:
                groups += [("v", n, b) for b in range(1, KC)]
            if c is not None:
                groups += [("t3", c, j) for j in range(NB)]
        misc_no = {g: i for i, g in enumerate(groups)}
        reader = {"u": g_ok, "t1": x1_lo, "v": v_ok, "o": h_ok, "t3": x3_lo}

        def bank(kind, t, i):
            return misc[misc_no[kind, t, i] % 2]

        def mean_var(ln):
            return mv[:, ln, :, :]

        def raw_stats(ln):
            return bn[:, ln, :, :]

        block = ctx.enter_context(nc.Block())

        @block.sync
        def _(sp):
            def load_x(t):
                if t >= X_SLOTS:
                    sp.wait_ge(fin_ok, NB * (t - X_SLOTS + 1))
                if t == 2:
                    sp.wait_ge(wo_l, KC)
                sp.dma_start(xs[:, t % X_SLOTS, :, :], x_d[t]).then_inc(x_in[t % X_SLOTS], 16)

            def load_chunk(i):
                if G_SLOTS <= i < NCH:
                    sp.wait_ge(abs_ok, i - G_SLOTS + 1)
                elif i >= NCH:
                    sp.wait_ge(abs_ok, min(i - G_SLOTS + 1, NCH))
                    if i - G_SLOTS >= NCH:
                        sp.wait_ge(w_ok, i - G_SLOTS - NCH + 1)
                sp.dma_start(gg[:, i % G_SLOTS, :], chunks[i % NCH]).then_inc(chunk_in[i % G_SLOTS], 16)

            def store(t, j):
                sp.wait_ge(fin_ok, NB * t + j + 1)
                sp.dma_start(out_d[t, j], hb[:, j, :]).then_inc(out_st[j], 16)

            load_x(0)
            sp.dma_start(vb[:, 0:KC * 2 * D].rearrange("p (k n) -> p k n", k=KC), w_in_d).then_inc(win_in, 16)
            sp.dma_start(par[:, :], params).then_inc(par_in, 16)
            load_x(1)
            sp.dma_start(xs[:, 2, :, :], w_out_d).then_inc(wout_in, 16)
            sp.dma_start(row[:, :, :], rows.partition_broadcast(P)).then_inc(row_in, 16)
            for i in range(NCH):
                load_chunk(i)
            load_x(2)
            load_x(3)
            for i in range(NCH, 2 * NCH):
                load_chunk(i)
            for s in STEPS:
                _, _, _, e = tiles(s)
                if e is not None:
                    for j in range(NB):
                        store(e, j)
                    if e + X_SLOTS < NT:
                        load_x(e + X_SLOTS)
            for j in range(NB):
                store(NT - 1, j)
            for j in range(NB):
                sp.wait_ge(out_st[j], 16 * NT)

        @block.tensor
        def _(pe):
            def take(kind, t, i):
                m = misc_no[kind, t, i]
                if m >= 2:
                    k, t0, i0 = groups[m - 2]
                    pe.wait_ge(reader[k], 4 * t0 + i0 + 1)
                return bank(kind, t, i)

            def transposes(kind, t, j, src, done):
                b = take(kind, t, j)
                for k in range(KC):
                    mm = pe.transpose(b[:, k * P:(k + 1) * P], src[:, k * P:(k + 1) * P], ident[:, :])
                mm.then_inc(done, 1)

            def t1(n, j):
                pe.wait_ge(xn_ok, NB * n + j + 1)
                transposes("t1", n, j, xn[:, j % 2, :], t1_mm)

            def t3(c, j):
                pe.wait_ge(n3_ok, NB * c + j + 1)
                transposes("t3", c, j, hb[:, j, :], t3_mm)

            def in_proj(kind, t, b, done):
                pe.wait_ge(x1_lo, NB * (t + 1))
                o = take(kind, t, b)
                c0_, s_ = (D if kind == "v" else 0) + b * P, t % 2
                for k in range(KC):
                    wh, wl = win_hi[:, k, c0_:c0_ + P], win_lo[:, k, c0_:c0_ + P]
                    pe.matmul(o[:, :], wh, x1T_hi[:, s_, k, :], start=k == 0, stop=False)
                    pe.matmul(o[:, :], wh, x1T_lo[:, s_, k, :], start=False, stop=False)
                    mm = pe.matmul(o[:, :], wl, x1T_hi[:, s_, k, :], start=False, stop=k == KC - 1)
                mm.then_inc(done, 1)

            def o(c, j):
                out_ = take("o", c, j)
                js = slice(j * P, (j + 1) * P)
                for k in range(KC):
                    pe.wait_ge(glo_ok, KC * c + k + 1)
                    pe.matmul(out_[:, :], g_hi[:, k, js], wo_hi[:, k, :], start=k == 0, stop=False)
                    pe.matmul(out_[:, :], g_hi[:, k, js], wo_lo[:, k, :], start=False, stop=False)
                    mm = pe.matmul(out_[:, :], g_lo[:, k, js], wo_hi[:, k, :], start=False, stop=k == KC - 1)
                mm.then_inc(o_mm, 1)

            def f1(t, j):
                i = FC * t + j
                if j == 0:
                    pe.wait_ge(x3_lo, NB * (t + 1))
                if i >= 2:
                    pe.wait_ge(gelu_ok, i - 1)
                b = f1b[i % 2]
                for k in range(KC):
                    w = w1[:, k, j * P:(j + 1) * P]
                    pe.matmul(b[:, :], w, x3T_hi[:, k, :], start=k == 0, stop=False)
                    mm = pe.matmul(b[:, :], w, x3T_lo[:, k, :], start=False, stop=k == KC - 1)
                mm.then_inc(f1_mm, 1)

            def f2(t, j):
                i = FC * t + j
                if j == 0 and t > 0:
                    pe.wait_ge(f_ok, NB * t)
                pe.wait_ge(hl_ok, i + 1)
                for q in range(NB):
                    qs = slice(q * P, (q + 1) * P)
                    pe.matmul(f2b[q][:, :], h_hi[:, i % H_SLOTS, qs], w2[:, j, :], start=j == 0, stop=False)
                    mm = pe.matmul(f2b[q][:, :], h_lo[:, i % H_SLOTS, qs], w2[:, j, :], start=False, stop=j == FC - 1)
                mm.then_inc(f2_mm, 1)

            pe.wait_ge(const_ok, 3)
            pe.wait_ge(pmx, 2)
            pe.transpose(misc[0][0:1, 0:P], wmax[:, 1:2], ident[:, :]).then_inc(pm1, 1)
            pe.wait_ge(pmx, 3)
            pe.matmul(misc[0][:, 256:257], ones[0:1, :], wrow[0:1, 0:1], start=True, stop=True).then_inc(pm1, 1)
            pe.wait_ge(pmx, 4)
            for s in STEPS:
                fa, c, n, _ = tiles(s)
                if fa is not None:
                    if fa == 0:
                        pe.wait_ge(w2_ok, FC)
                    for j in range(HALF):
                        f1(fa, j)
                        if j >= LAG:
                            f2(fa, j - LAG)
                    for j in range(HALF - LAG, HALF):
                        f2(fa, j)
                if c is not None:
                    for b in range(KC):
                        in_proj("u", c, b, u_mm)
                if n is not None:
                    for j in range(NB):
                        t1(n, j)
                    if n == 0:
                        pe.wait_ge(win_l, 2 * KC)
                    in_proj("v", n, 0, v_mm)
                if c is not None:
                    if c == 0:
                        pe.wait_ge(wo_l, KC)
                    for j in range(NB):
                        o(c, j)
                if n is not None:
                    for b in range(1, KC):
                        in_proj("v", n, b, v_mm)
                if s == 0:
                    pe.wait_ge(thr_ok, 1)
                    pe.matmul(f2b[0][:, 0:2], ones[:, :], thr_s[:, :], start=True, stop=True).then_inc(thr_mm, 1)
                if fa is not None:
                    for j in range(HALF, FC):
                        f1(fa, j)
                        if j >= HALF + LAG:
                            f2(fa, j - LAG)
                if c is not None:
                    t3(c, 0)
                if fa is not None:
                    f2(fa, FC - 2)
                if c is not None:
                    t3(c, 1)
                    t3(c, 2)
                if fa is not None:
                    f2(fa, FC - 1)
                if c is not None:
                    t3(c, 3)

        @block.vector
        def _(ve_):
            chain = [0]

            def link(ins):
                ins.then_inc(prep, 1)
                chain[0] += 1
                ve_.wait_ge(prep, chain[0])

            def stats(ln, t, j, src):
                if t > 0:
                    ve_.wait_ge(mv_ok[ln], NB * (t - 1) + j + 1)
                ve_.bn_stats(raw_stats(ln)[:, j, :], src).then_inc(bn_ok[ln], 1)

            def aggr(ln, t, j):
                ve_.wait_ge(bn_ok[ln], NB * t + j + 1)
                if t > 0:
                    ve_.wait_ge(rs_ok[ln], t)
                ve_.bn_aggr(mean_var(ln)[:, j, :], raw_stats(ln)[:, j, :]).then_inc(mv_ok[ln], 1)

            def lo(t, j):
                i = FC * t + j
                ve_.wait_ge(hh_ok, i + 1)
                ve_.scalar_tensor_tensor(out=h_lo[:, i % H_SLOTS, :], in0=gg[:, i % G_SLOTS, :],
                                         scalar=f_sc[:, j:j + 1], in1=h_hi[:, i % H_SLOTS, :],
                                         op0=ALU.mult, op1=ALU.subtract).then_inc(hl_ok, 1)

            def f_add(e, j):
                if j == 0:
                    ve_.wait_ge(f2_mm, FC * (e + 1))
                if e + 1 < NT:
                    ve_.wait_ge(t3_mm, NB * (e + 1) + j + 1)
                else:
                    ve_.wait_ge(out_st[j], 16 * e)
                ve_.tensor_tensor(hb[:, j, :], f2b[j][:, :], b2_row, ALU.add).then_inc(f_ok, 1)

            def f_stats(e, j):
                ve_.wait_ge(f_ok, NB * e + j + 1)
                stats(4, e, j, hb[:, j, :])

            def epilogue(e):
                return (spread(AT_F_ADD, .2, [lambda j=j: f_add(e, j) for j in range(NB)])
                        + spread(AT_F_STATS, .2, [lambda j=j: f_stats(e, j) for j in range(NB)])
                        + spread(AT_F_AGGR, .05, [lambda j=j: aggr(4, e, j) for j in range(NB)]))

            def ln1(n):
                def st(j):
                    if j == 0:
                        ve_.wait_ge(x_in[n % X_SLOTS], 16 * (n // X_SLOTS + 1))
                    stats(0, n, j, xs[:, n % X_SLOTS, j, :])
                return (spread(AT_LN1, .2, [lambda j=j: st(j) for j in range(NB)])
                        + spread(AT_LN1 + .8, .05, [lambda j=j: aggr(0, n, j) for j in range(NB)]))

            def conv_scan(c):
                def taps(b, first):
                    i = KC * c + b
                    if first:
                        ve_.wait_ge(tap1, i + 1)
                        if b == 0:
                            ve_.wait_ge(left_ok, c + 1)
                            ve_.wait_ge(right_ok, c + 1)
                        src, w, done = v[:, c % 2, b, 0:TT], par[:, CW + b:CW + b + 1], tap0
                    else:
                        ve_.wait_ge(tap0, i + 1)
                        src, w, done = v[:, c % 2, b, 2:TT + 2], par[:, CW + 8 + b:CW + 9 + b], tap2
                    dst = vl[:, i % 2, :]
                    ve_.scalar_tensor_tensor(out=dst, in0=src, scalar=w, in1=dst,
                                             op0=ALU.mult, op1=ALU.add).then_inc(done, 1)

                def scan(b):
                    i = KC * c + b
                    ve_.wait_ge(tap2, i + 1)
                    if i >= 2:
                        ve_.wait_ge(y_ok, i - 1)
                        ve_.wait_ge(carry_ok, i - 1)
                    if c > 0:
                        ve_.wait_ge(carry_ok, i - KC + 1)
                    ve_.tensor_tensor_scan(out=ss[:, i % 2, :], data0=a_par[:, b:b + 1].to_broadcast([P, TT]),
                                           data1=vl[:, i % 2, :],
                                           initial=carry[:, b:b + 1] if c > 0 else 0.0,
                                           op0=ALU.mult, op1=ALU.add).then_inc(scan_ok, 1)

                def y(b):
                    i = KC * c + b
                    ve_.wait_ge(scan_ok, i + 1)
                    ve_.wait_ge(dv_ok, i + 1)
                    dst = yb[:, b, :]
                    ve_.scalar_tensor_tensor(out=dst, in0=ss[:, i % 2, :], scalar=cb_par[:, b:b + 1], in1=dst,
                                             op0=ALU.mult, op1=ALU.add).then_inc(y_ok, 1)

                items = []
                for b, at in zip(range(0, KC, 2), AT_PAIR):
                    items += spread(at, .2, [lambda b=b: taps(b, True), lambda b=b: taps(b + 1, True),
                                             lambda b=b: taps(b, False), lambda b=b: taps(b + 1, False)])
                    items += spread(at + .9, .4, [lambda b=b: scan(b), lambda b=b: scan(b + 1)])
                    items += spread(at + 1.6, .2, [lambda b=b: y(b), lambda b=b: y(b + 1)])
                return items

            def gate(c, b):
                i = KC * c + b
                ve_.wait_ge(sy_ok, i + 1)
                ve_.wait_ge(u_mm, i + 1)
                dst = yb[:, b, :]
                ve_.scalar_tensor_tensor(out=dst, in0=bank("u", c, b)[:, :], scalar=bu_sig[:, b:b + 1], in1=dst,
                                         op0=ALU.add, op1=ALU.mult).then_inc(g_ok, 1)

            def gate_lo(c, b):
                ve_.wait_ge(ghi_ok, KC * c + b + 1)
                ve_.tensor_tensor(g_lo[:, b, :], yb[:, b, :], g_hi[:, b, :].bitcast(F32),
                                  ALU.subtract).then_inc(glo_ok, 1)

            def t_lo(kind, t, j):
                hi, lo_, ok, done = ((x1T_hi[:, t % 2], x1T_lo[:, t % 2], x1_hi, x1_lo) if kind == "t1"
                                     else (x3T_hi, x3T_lo, x3_hi, x3_lo))
                ve_.wait_ge(ok, NB * t + j + 1)
                js = slice(j * P, (j + 1) * P)
                ve_.scalar_tensor_tensor(out=lo_[:, :, js], in0=bank(kind, t, j)[:, :].rearrange("p (k t) -> p k t", k=KC),
                                         scalar=ACT_SCALE, in1=hi[:, :, js],
                                         op0=ALU.mult, op1=ALU.subtract).then_inc(done, 1)

            def h_add(c, j):
                ve_.wait_ge(o_mm, NB * c + j + 1)
                ve_.wait_ge(resb_ok, NB * c + j + 1)
                ve_.scalar_tensor_tensor(out=hb[:, j, :], in0=bank("o", c, j)[:, :], scalar=inv_sig[:, 0:1],
                                         in1=hb[:, j, :], op0=ALU.mult, op1=ALU.add).then_inc(h_ok, 1)

            def h_stats(c, j):
                ve_.wait_ge(h_ok, NB * c + j + 1)
                stats(1, c, j, hb[:, j, :])

            def norms(c):
                xsl = xs[:, c % X_SLOTS]

                def a1(j):
                    if j == 0:
                        ve_.wait_ge(rs_ok[1], c + 1)
                    ve_.scalar_tensor_tensor(out=hb[:, j, :], in0=hb[:, j, :], scalar=mean_var(1)[:, j, 0:1],
                                             in1=lnw_row, op0=ALU.subtract, op1=ALU.mult).then_inc(a1_ok, 1)

                def a2(j):
                    ve_.wait_ge(a1_ok, NB * c + j + 1)
                    ve_.scalar_tensor_tensor(out=hb[:, j, :], in0=hb[:, j, :], scalar=rsc[:, 0, j:j + 1],
                                             in1=lnb_row, op0=ALU.mult, op1=ALU.add).then_inc(a2_ok, 1)

                def b_stats(j):
                    ve_.wait_ge(a2_ok, NB * c + j + 1)
                    stats(2, c, j, hb[:, j, :])

                def x1(j):
                    if j == 0:
                        ve_.wait_ge(rs_ok[2], c + 1)
                    ve_.scalar_tensor_tensor(out=xsl[:, j, :], in0=hb[:, j, :], scalar=rsc[:, 1, j:j + 1],
                                             in1=xsl[:, j, :], op0=ALU.mult, op1=ALU.add).then_inc(x1_ok, 1)

                def c_stats(j):
                    ve_.wait_ge(x1_ok, NB * c + j + 1)
                    stats(3, c, j, xsl[:, j, :])

                def n3(j):
                    if j == 0:
                        ve_.wait_ge(rs_ok[3], c + 1)
                    ve_.tensor_scalar(hb[:, j, :], xsl[:, j, :], mean_var(3)[:, j, 0:1], rsc[:, 2, j:j + 1],
                                      ALU.subtract, ALU.mult).then_inc(n3_ok, 1)

                kinds = [a1, a2, b_stats, lambda j: aggr(2, c, j), x1, c_stats, lambda j: aggr(3, c, j), n3]
                return spread(AT_NORMS, .2, [lambda f=f, j=j: f(j) for f in kinds for j in range(NB)])

            def setup_in_proj():
                wf = vb[:, 0:KC * 2 * D]
                ve_.wait_ge(win_in, 16)
                ve_.tensor_reduce(wmax[:, 0:1], wf, AX.X, ALU.max, apply_absolute_value=True).then_inc(pmx, 1)
                ve_.wait_ge(pmx, 1)
                ve_.tensor_scalar(wmax[:, 1:2].bitcast(U32), wmax[:, 0:1].bitcast(U32), 0x7F800000, None,
                                  ALU.bitwise_and).then_inc(pmx, 1)
                ve_.wait_ge(pm1, 1)
                ve_.tensor_reduce(wrow[0:1, 0:1], misc[0][0:1, 0:P], AX.X, ALU.max).then_inc(pmx, 1)
                ve_.wait_ge(pm1, 2)
                ve_.tensor_scalar(wmax[:, 2:3], misc[0][:, 256:257], 2.0 ** -100, 2.0 ** -13,
                                  ALU.max, ALU.mult).then_inc(pmx, 1)
                ve_.wait_ge(pmx, 4)
                link(ve_.reciprocal(wmax[:, 3:4], wmax[:, 2:3]))
                link(ve_.tensor_scalar(inv_sig[:, :], wmax[:, 2:3], 1.0 / ACT_SCALE, None, ALU.mult))
                link(ve_.tensor_scalar(sig[:, :], wmax[:, 3:4], ACT_SCALE, None, ALU.mult))
                for i in range(2 * KC):
                    k, hs = i % KC, (D if i < KC else 0)
                    ve_.wait_ge(win_h, i + 1)
                    ve_.scalar_tensor_tensor(out=win_lo[:, k, hs:hs + D], in0=wf[:, k * 2 * D + hs:k * 2 * D + hs + D],
                                             scalar=wmax[:, 3:4], in1=win_hi[:, k, hs:hs + D],
                                             op0=ALU.mult, op1=ALU.subtract).then_inc(win_l, 1)

            def setup_params():
                ve_.wait_ge(par_in, 16)
                link(ve_.tensor_scalar(bu_sig[:, :], par[:, BIN:BIN + KC], sig[:, 0:1], None, ALU.mult))
                link(ve_.tensor_tensor(cb_par[:, :], par[:, SC:SC + KC], par[:, SB:SB + KC], ALU.mult))
                ve_.wait_ge(tanh_ok, 1)
                ve_.tensor_scalar(a_par[:, :], a_par[:, :], 1.0, 0.5, ALU.add, ALU.mult).then_inc(a_ok, 1)
                ve_.wait_ge(a_ok, 1)
                link(ve_.tensor_scalar(f_inv[:, :].bitcast(U32), par[:, B1:B1 + FC].bitcast(U32), 0x7FFFFFFF, None,
                                       ALU.bitwise_and))
                link(ve_.tensor_scalar(f_sc[:, :], f_inv[:, :], 512.0, None, ALU.add))
                link(ve_.tensor_scalar(f_inv[:, :].bitcast(U32), f_sc[:, :].bitcast(U32), 0x7F800000, None,
                                       ALU.bitwise_and))
                link(ve_.tensor_scalar(f_inv[:, :], f_inv[:, :], 2.0 ** -14, None, ALU.mult))
                link(ve_.reciprocal(f_sc[:, :], f_inv[:, :]))

            def setup_out_proj(k):
                ve_.wait_ge(wo_h, k + 1)
                ve_.tensor_tensor(wo_lo[:, k, :], xs[:, 2, k, :], wo_hi[:, k, :].bitcast(F32),
                                  ALU.subtract).then_inc(wo_l, 1)

            def setup_thresholds():
                ve_.wait_ge(abs_ok, NCH)
                link(ve_.tensor_reduce(thr_s[:, 0:1], asum[:, 0:NCH // 2], AX.X, ALU.add))
                ve_.tensor_reduce(thr_s[:, 1:2], asum[:, NCH // 2:NCH], AX.X, ALU.add).then_inc(thr_ok, 1)
                ve_.wait_ge(thr_mm, 1)
                link(ve_.tensor_scalar(thr[:, 0:2], f2b[0][:, 0:2], 1.0 / (D * FF), 1e-8, ALU.mult, ALU.max))
                link(ve_.tensor_scalar(thr[:, 0:2], thr[:, 0:2], 0.5, None, ALU.mult))
                ve_.tensor_scalar(thr[:, 2:4], thr[:, 0:2], -1.0, None, ALU.mult).then_inc(thr_ok, 1)
                ve_.wait_ge(thr_ok, 2)

            def ternary(i):
                m = i // (NCH // 2)
                src = gg[:, (NCH + i) % G_SLOTS, :]
                dst = w1[:, i // NQ, (i % NQ) * 512:(i % NQ) * 512 + 512] if m == 0 else w2[:, i - NCH // 2, :]
                ve_.wait_ge(t_ok, i + 1)
                ve_.scalar_tensor_tensor(out=dst, in0=src, scalar=thr[:, m:m + 1], in1=h_hi[:, i % 2, :],
                                         op0=ALU.is_gt, op1=ALU.add).then_inc(w_ok, 1)

            run(ln1(0))
            setup_in_proj()
            for s in STEPS:
                fa, c, n, e = tiles(s)
                items = []
                if e is not None:
                    items += epilogue(e)
                if n is not None and n > 0:
                    items += ln1(n)
                if c is not None:
                    items += conv_scan(c)
                if fa is not None:
                    items += spread(1.2, 1, [lambda j=j: lo(fa, j) for j in range(HALF)])
                if s == 1:
                    items += spread(0, AT_LN1 / NCH, [lambda i=i: ternary(i) for i in range(NCH)])
                run(items)
                if c is not None:
                    gate(c, 0)
                    for b in range(1, KC):
                        gate(c, b)
                        gate_lo(c, b - 1)
                    gate_lo(c, KC - 1)
                if n is not None:
                    for j in range(NB):
                        t_lo("t1", n, j)
                if s == -1:
                    setup_params()
                if s == 0:
                    for k in range(KC):
                        setup_out_proj(k)
                    setup_thresholds()
                items = []
                if c is not None:
                    for j in range(NB):
                        h_add(c, j)
                        if j:
                            h_stats(c, j - 1)
                            if j > 1:
                                aggr(1, c, j - 2)
                    h_stats(c, NB - 1)
                    aggr(1, c, NB - 2)
                    aggr(1, c, NB - 1)
                    items = norms(c)
                if fa is not None:
                    items += spread(HALF + 1.2, 1, [lambda j=j: lo(fa, j) for j in range(HALF, FC)])
                run(items)
                if c is not None:
                    for j in range(NB):
                        t_lo("t3", c, j)
            run(epilogue(NT - 1))

        @block.scalar
        def _(act):
            def gelu(t, j):
                i = FC * t + j
                act.wait_ge(f1_mm, i + 1)
                if i >= G_SLOTS:
                    act.wait_ge(hl_ok, i - G_SLOTS + 1)
                act.activation(gg[:, i % G_SLOTS, :], f1b[i % 2][:, :], ACT.Gelu,
                               bias=par[:, B1 + j:B1 + j + 1], scale=1.0 / ACT_SCALE).then_inc(gelu_ok, 1)

            def hi(t, j):
                i = FC * t + j
                act.wait_ge(gelu_ok, i + 1)
                if i >= H_SLOTS:
                    act.wait_ge(f2_mm, i - H_SLOTS + 1)
                act.activation(h_hi[:, i % H_SLOTS, :], gg[:, i % G_SLOTS, :], ACT.Copy,
                               scale=f_sc[:, j:j + 1]).then_inc(hh_ok, 1)

            def ffn(t, js):
                return (spread(js[0], 1, [lambda j=j: gelu(t, j) for j in js])
                        + spread(js[0] + 1.1, 1, [lambda j=j: hi(t, j) for j in js]))

            def ffn_norm(e, j):
                if j == 0:
                    act.wait_ge(rs_ok[4], e + 1)
                act.activation(hb[:, j, :], hb[:, j, :], ACT.Identity, bias=nm4[:, j:j + 1],
                               scale=rs4[:, j:j + 1]).then_inc(fn_ok, 1)

            def centre_tap(c, b):
                i = KC * c + b
                act.wait_ge(v_ok, i + 1)
                if i >= 2:
                    act.wait_ge(scan_ok, i - 1)
                    act.wait_ge(dv_ok, i - 1)
                act.activation(vl[:, i % 2, :], v[:, c % 2, b, 1:TT + 1], ACT.Identity,
                               bias=par[:, CB + b:CB + b + 1], scale=par[:, CW + 4 + b:CW + 5 + b]).then_inc(tap1, 1)

            def d_conv(c, b):
                i = KC * c + b
                act.wait_ge(tap2, i + 1)
                if c > 0:
                    act.wait_ge(glo_ok, i - KC + 1)
                act.activation(yb[:, b, :], vl[:, i % 2, :], ACT.Copy,
                               scale=par[:, SD + b:SD + b + 1]).then_inc(dv_ok, 1)

            def residual(c, j):
                if c > 0:
                    act.wait_ge(t3_mm, NB * (c - 1) + j + 1)
                if c > 1:
                    act.wait_ge(out_st[j], 16 * (c - 1))
                act.activation(hb[:, j, :], xs[:, c % X_SLOTS, j, :], ACT.Identity, bias=nm1[:, c % 4, j:j + 1],
                               scale=rs1[:, c % 4, j:j + 1]).then_inc(res_ok, 1)

            def silu_y(c, b):
                act.wait_ge(y_ok, KC * c + b + 1)
                act.activation(yb[:, b, :], yb[:, b, :], ACT.Silu).then_inc(sy_ok, 1)

            def gate_hi(c, b):
                act.wait_ge(g_ok, KC * c + b + 1)
                if b == 0 and c > 0:
                    act.wait_ge(o_mm, NB * c)
                act.activation(g_hi[:, b, :], yb[:, b, :], ACT.Copy).then_inc(ghi_ok, 1)

            def norm_x(n, j):
                i = NB * n + j
                if j == 0:
                    act.wait_ge(rs_ok[0], n + 1)
                if i >= 2:
                    act.wait_ge(t1_mm, i - 1)
                act.activation(xn[:, i % 2, :], xs[:, n % X_SLOTS, j, :], ACT.Identity, bias=nm1[:, n % 4, j:j + 1],
                               scale=rs1[:, n % 4, j:j + 1]).then_inc(xn_ok, 1)

            def t_hi(kind, t, j):
                if kind == "t1":
                    hi_, mm, done = x1T_hi[:, t % 2], t1_mm, x1_hi
                    if t > 1 and j == 0:
                        act.wait_ge(u_mm, KC * (t - 1))
                else:
                    hi_, mm, done = x3T_hi, t3_mm, x3_hi
                    if t > 0 and j == 0:
                        act.wait_ge(f1_mm, FC * t)
                act.wait_ge(mm, NB * t + j + 1)
                act.activation(hi_[:, :, j * P:(j + 1) * P], bank(kind, t, j)[:, :].rearrange("p (k t) -> p k t", k=KC),
                               ACT.Copy, scale=ACT_SCALE).then_inc(done, 1)

            def silu_v(n, b):
                act.wait_ge(v_mm, KC * n + b + 1)
                if n > 1 and b == 0:
                    act.wait_ge(tap2, KC * (n - 1))
                if n == 0 and b == 0:
                    act.wait_ge(win_l, 2 * KC)
                if n > 0 and b == 0:
                    act.wait_ge(left_ok, n)
                    if n > 1:
                        act.wait_ge(right_ok, n - 1)
                act.activation(v[:, n % 2, b, 1:TT + 1], bank("v", n, b)[:, :], ACT.Silu,
                               bias=par[:, BIN + KC + b:BIN + KC + b + 1], scale=inv_sig[:, 0:1]).then_inc(v_ok, 1)

            def abs_sum(i):
                act.wait_ge(chunk_in[i % G_SLOTS], 16 * (i // G_SLOTS + 1))
                if i >= KC:
                    act.wait_ge(abs_ok, i - KC + 1)
                act.activation(yb[:, i % KC, :], gg[:, i % G_SLOTS, :], ACT.Abs,
                               accum_out=asum[:, i:i + 1]).then_inc(abs_ok, 1)

            act.wait_ge(par_in, 16)
            act.activation(a_par[:, :], par[:, LA:LA + KC], ACT.Tanh, scale=0.5).then_inc(tanh_ok, 1)
            for s in STEPS:
                fa, c, n, e = tiles(s)
                items = []
                if e is not None:
                    items += spread(AT_F_NORM, .2, [lambda j=j: ffn_norm(e, j) for j in range(NB)])
                if c is not None:
                    for b, at in zip(range(0, KC, 2), AT_PAIR):
                        items += spread(at - .3, .15, [lambda b=b: centre_tap(c, b), lambda b=b: centre_tap(c, b + 1)])
                        items += spread(at + 1.0, .4, [lambda b=b: d_conv(c, b), lambda b=b: d_conv(c, b + 1)])
                    items += spread(AT_RES, .2, [lambda j=j: residual(c, j) for j in range(NB)])
                if fa is not None:
                    items += ffn(fa, range(HALF))
                run(items)
                if c is not None:
                    for b in range(KC):
                        silu_y(c, b)
                if s == -1:
                    for j in range(2):
                        norm_x(n, j)
                    act.wait_ge(prep, 1)
                    for i in range(2 * KC):
                        k, hs = i % KC, (D if i < KC else 0)
                        act.activation(win_hi[:, k, hs:hs + D], vb[:, k * 2 * D + hs:k * 2 * D + hs + D], ACT.Copy,
                                       scale=wmax[:, 3:4]).then_inc(win_h, 1)
                order = []
                gh = [lambda b=b: gate_hi(c, b) for b in range(KC)] if c is not None else []
                xj = [lambda j=j: norm_x(n, j) for j in range(NB)] if n is not None else []
                th = [lambda j=j: t_hi("t1", n, j) for j in range(NB)] if n is not None else []
                if s == -1:
                    order = th[:1] + xj[2:3] + th[1:2] + xj[3:] + th[2:]
                else:
                    order = gh[:1] + xj[:1] + gh[1:2] + xj[1:2] + gh[2:] + th[:1] + xj[2:3] + th[1:2] + xj[3:] + th[2:]
                for item in order:
                    item()
                if n is not None:
                    for b in range(KC):
                        silu_v(n, b)
                if s == 0:
                    act.wait_ge(wout_in, 16)
                    for k in range(KC):
                        act.activation(wo_hi[:, k, :], xs[:, 2, k, :], ACT.Copy).then_inc(wo_h, 1)
                    for i in range(NCH):
                        abs_sum(i)
                if fa is not None:
                    run(ffn(fa, range(HALF, FC)))
                if c is not None:
                    for j in range(NB):
                        t_hi("t3", c, j)
            for j in range(NB):
                ffn_norm(NT - 1, j)

        @block.gpsimd
        def _(pool):
            chain = [0]

            def link(ins):
                ins.then_inc(pool_ok, 1)
                chain[0] += 1
                pool.wait_ge(pool_ok, chain[0])

            def rstd(ln, t, dst, last):
                pool.wait_ge(mv_ok[ln], NB * (t + 1))
                link(pool.tensor_scalar(ve[:, ln, :], mean_var(ln)[:, :, 1], EPS, None, ALU.add))
                ins = pool.tensor_tensor(dst, ve[:, ln, :], mhalf[:, :], ALU.pow)
                if last:
                    ins.then_inc(rs_ok[ln], 1)
                else:
                    link(ins)

            def rstd_x(n):
                if n > 3:
                    pool.wait_ge(res_ok, NB * (n - 3))
                rstd(0, n, rs1[:, n % 4, :], False)
                link(pool.tensor_tensor(tmp4[:, 0, :], mean_var(0)[:, :, 0], rs1[:, n % 4, :], ALU.mult))
                pool.tensor_scalar(nm1[:, n % 4, :], tmp4[:, 0, :], -1.0, None, ALU.mult).then_inc(rs_ok[0], 1)

            def rstd_b(c):
                rstd(2, c, rsc[:, 1, :], False)
                pool.tensor_tensor(c0[:, c % 4, :], mean_var(2)[:, :, 0], rsc[:, 1, :], ALU.mult).then_inc(rs_ok[2], 1)

            def rstd_f(e):
                if e > 0:
                    pool.wait_ge(fn_ok, NB * e)
                rstd(4, e, rs4[:, :], False)
                link(pool.tensor_tensor(tmp4[:, 1, :], mean_var(4)[:, :, 0], rs4[:, :], ALU.mult))
                link(pool.tensor_tensor(tmp4[:, 2, :], tmp4[:, 1, :], c0[:, e % 4, :], ALU.add))
                pool.tensor_scalar(nm4[:, :], tmp4[:, 2, :], -1.0, None, ALU.mult).then_inc(rs_ok[4], 1)

            def finish(e, j):
                pool.wait_ge(fn_ok, NB * e + j + 1)
                pool.tensor_tensor(hb[:, j, :], hb[:, j, :], xs[:, e % X_SLOTS, j, :], ALU.add).then_inc(fin_ok, 1)

            def keep_state(c, b):
                i = KC * c + b
                pool.wait_ge(scan_ok, i + 1)
                pool.tensor_copy(carry[:, b:b + 1], ss[:, i % 2, TT - 1:TT]).then_inc(carry_ok, 1)

            def add_bias(c, j):
                pool.wait_ge(res_ok, NB * c + j + 1)
                pool.tensor_tensor(hb[:, j, :], hb[:, j, :], ob_row, ALU.add).then_inc(resb_ok, 1)

            def edges(n):
                if n < NT:
                    pool.wait_ge(v_ok, KC * (n + 1))
                if n == 0:
                    pool.memset(v[:, 0, :, 0:1], 0.0).then_inc(left_ok, 1)
                    return
                if n < NT:
                    if n > 1:
                        pool.wait_ge(tap2, KC * (n - 1))
                    pool.tensor_copy(v[:, n % 2, :, 0:1], v[:, (n - 1) % 2, :, TT:TT + 1]).then_inc(left_ok, 1)
                    pool.tensor_copy(v[:, (n - 1) % 2, :, TT + 1:TT + 2], v[:, n % 2, :, 1:2]).then_inc(right_ok, 1)
                else:
                    pool.memset(v[:, (n - 1) % 2, :, TT + 1:TT + 2], 0.0).then_inc(right_ok, 1)

            def ternary_low(i):
                m = i // (NCH // 2)
                q = NCH + i
                pool.wait_ge(chunk_in[q % G_SLOTS], 16 * (q // G_SLOTS + 1))
                if i >= 2:
                    pool.wait_ge(w_ok, i - 1)
                pool.tensor_scalar(h_hi[:, i % 2, :], gg[:, q % G_SLOTS, :], thr[:, 2 + m:3 + m], 1.0,
                                   ALU.is_ge, ALU.subtract).then_inc(t_ok, 1)

            def scale_w2(j):
                pool.wait_ge(w_ok, NCH // 2 + j + 1)
                pool.tensor_scalar(w2[:, j, :], w2[:, j, :], f_inv[:, j:j + 1], None, ALU.mult).then_inc(w2_ok, 1)

            pool.memset(ident[:, :], 0.0).then_inc(const_ok, 1)
            pool.memset(ones[:, :], 1.0).then_inc(const_ok, 1)
            pool.wait_ge(const_ok, 2)
            pool.affine_select(out=ident[:, :], in_=ident[:, :], compare_op=ALU.not_equal, fill=1.0, base=0,
                               pattern=[[-1, P]], channel_multiplier=1).then_inc(const_ok, 1)
            link(pool.memset(mhalf[:, :], -0.5))
            for s in STEPS:
                fa, c, n, e = tiles(s)
                if e is not None:
                    rstd_f(e)
                    for j in range(NB):
                        finish(e, j)
                items = []
                if c is not None:
                    for b, at in zip(range(0, KC, 2), AT_PAIR):
                        items += spread(at + 1.0, .4, [lambda b=b: keep_state(c, b), lambda b=b: keep_state(c, b + 1)])
                if s == 1:
                    pool.wait_ge(row_in, 16)
                    pool.wait_ge(thr_ok, 2)
                    items += spread(-.01, AT_LN1 / NCH, [lambda i=i: ternary_low(i) for i in range(NCH)])
                if n is not None:
                    items.append((AT_LN1 + 1, lambda: rstd_x(n)))
                run(items)
                if c is not None:
                    for j in range(NB):
                        add_bias(c, j)
                    if s == 1:
                        for j in range(FC):
                            scale_w2(j)
                    rstd(1, c, rsc[:, 0, :], True)
                    rstd_b(c)
                    rstd(3, c, rsc[:, 2, :], True)
                if n is not None:
                    edges(n)
                if s == NT - 1:
                    edges(NT)
            rstd_f(NT - 1)
            for j in range(NB):
                finish(NT - 1, j)


def kernel(**inputs):
    import numpy as np
    import concourse.bacc as bacc
    from concourse.bass_utils import run_bass_kernel_spmd

    def get(name):
        return np.asarray(inputs[name])

    x = get("L0_attn_x")
    cols = [get("L0_attn_in_proj_b").reshape(-1, P)]
    cols += [get("L0_attn_conv_w")[:, 0, k].reshape(-1, P) for k in range(3)]
    cols += [get("L0_attn_" + n).reshape(-1, P) for n in ("conv_b", "logit_a", "ssm_b", "ssm_c", "ssm_d")]
    cols += [get("L0_ffn_b1").reshape(-1, P)]
    arrays = {
        "x_dram": x.reshape(-1, D),
        "w_in_dram": get("L0_attn_in_proj_w"),
        "w_out_dram": get("L0_attn_out_proj_w"),
        "w1t_dram": get("L0_ffn_W1").T,
        "w2t_dram": get("L0_ffn_W2").T,
        "params_dram": np.concatenate(cols, axis=0).T,
        "rows_dram": np.stack([get("L0_attn_out_proj_b"), get("L0_attn_ln_w"), get("L0_attn_ln_b"), get("L0_ffn_b2")]),
    }
    arrays = {n: np.ascontiguousarray(a) for n, a in arrays.items()}
    nc = bacc.Bacc("TRN2", target_bir_lowering=False, num_devices=1)
    args = [nc.dram_tensor(n, a.shape, mybir.dt.from_np(a.dtype), kind="ExternalInput").ap() for n, a in arrays.items()]
    out = nc.dram_tensor("out_dram", arrays["x_dram"].shape, F32, kind="ExternalOutput").ap()
    build(nc, *args, out)
    r = run_bass_kernel_spmd(nc, [arrays], core_ids=[0])
    return r.results[0]["out_dram"].reshape(x.shape)
```

```python
from contextlib import ExitStack

import concourse.bass as bass
from concourse import mybir

P = 128
D = 512
TT = 512
NB = TT // P
KC = D // P
LAG = 3
X_SLOTS = 4
G_SLOTS = 3
H_SLOTS = 4
EPS = 1e-5
ACT_SCALE = 2048.0

F32 = mybir.dt.float32
F32R = mybir.dt.float32r
F16 = mybir.dt.float16
U32 = mybir.dt.uint32
ALU = mybir.AluOpType
ACT = mybir.ActivationFunctionType
AX = mybir.AxisListType

BIN, CW, CB, LA, SB, SC, SD, B1 = 0, 8, 20, 24, 28, 32, 36, 40
NPAR = 56
W_SLOTS = NB


AT_F_ADD, AT_F_STATS, AT_F_AGGR = 0.0, 0.8, 1.6
AT_F_NORM = (2.7, 3.3, 4.4, 5.0)
AT_PAIR = (2.2, 5.0)
AT_LN1 = 9.0
AT_NORMS = 8.0


def at_w2(j):
    return .55 * max(j - W_SLOTS + 1, 0)


def run(items):
    for _, work in sorted(items, key=lambda item: item[0]):
        work()


def spread(at, step, works):
    return [(at + step * i, w) for i, w in enumerate(works)]


def build(nc, x, w_in, w_out, w1t, w2t, params, rows, out):
    T = x.shape[0]
    NT = T // TT
    FF = w1t.shape[1]
    FC = FF // P
    HALF = 9 * FC // 16
    STEPS = range(-1, NT + 2)

    x_d = x.rearrange("(t j p) d -> t p j d", p=P, j=NB)
    out_d = out.rearrange("(t j p) d -> t j p d", p=P, j=NB)
    w_in_d = w_in.rearrange("(k p) n -> p k n", p=P)
    w_out_d = w_out.rearrange("(k p) n -> p k n", p=P)
    w1_d = w1t.rearrange("(k p) (q n) -> k q p n", p=P, n=512)
    w2_d = w2t.rearrange("(c p) n -> c p n", p=P)
    NQ = FF // 512
    chunks = [w1_d[i // NQ, i % NQ] for i in range(KC * NQ)] + [w2_d[c] for c in range(FC)]
    NCH = len(chunks)

    with ExitStack() as ctx:
        def sb(name, shape, dt=F32):
            return ctx.enter_context(nc.sbuf_tensor(name, shape, dt))

        def sem(name):
            return ctx.enter_context(nc.semaphore(name))

        win_hi = sb("win_hi", [P, KC, 2 * D], F16)
        win_lo = sb("win_lo", [P, KC, 2 * D], F16)
        wo_hi = sb("wo_hi", [P, KC, D], F32R)
        wo_lo = sb("wo_lo", [P, KC, D], F32R)
        w1 = sb("w1", [P, KC, FF], F16)
        w2 = sb("w2", [P, FC, D], F16)
        row = sb("row", [P, 4, D])
        ob_row, lnw_row, lnb_row, b2_row = (row[:, i, :] for i in range(4))
        ident = sb("ident", [P, P])
        par = sb("par", [P, NPAR])
        xs = sb("xs", [P, X_SLOTS, NB, D])
        xn = sb("xn", [P, 2, D])
        hb = sb("hb", [P, NB, D])
        x1T_hi = sb("x1T_hi", [P, 2, KC, TT], F16)
        x1T_lo = sb("x1T_lo", [P, 2, KC, TT], F16)
        x3T_hi = sb("x3T_hi", [P, KC, TT], F16)
        x3T_lo = sb("x3T_lo", [P, KC, TT], F16)
        vb = sb("vb", [P, 2 * KC * (TT + 2)])
        v = vb[:, :].rearrange("p (s k t) -> p s k t", s=2, k=KC)
        wf = vb[:, 0:KC * 2 * D].rearrange("p (k n) -> p k n", k=KC)
        vl = sb("vl", [P, 2, TT])
        ss = sb("ss", [P, 2, TT])
        yb = sb("yb", [P, KC, TT])
        g_hi = sb("g_hi", [P, KC, TT], F32R)
        g_lo = sb("g_lo", [P, KC, TT], F32R)
        gg = sb("gg", [P, G_SLOTS, TT])
        wch = xs[:, X_SLOTS - 1]
        h_hi = sb("h_hi", [P, H_SLOTS, TT], F16)
        h_lo = sb("h_lo", [P, H_SLOTS, TT], F16)
        bn = sb("bn", [P, 5, NB, 6])
        mv = sb("mv", [P, 5, NB, 2])
        ve = sb("ve", [P, 5, NB])
        rs1 = sb("rs1", [P, 4, NB])
        nm1 = sb("nm1", [P, 4, NB])
        rsc = sb("rsc", [P, 3, NB])
        c0 = sb("c0", [P, 4, NB])
        rs4 = sb("rs4", [P, NB])
        nm4 = sb("nm4", [P, NB])
        mhalf = sb("mhalf", [P, NB])
        carry = sb("carry", [P, KC])
        tmp4 = sb("tmp4", [P, 3, NB])
        ones = sb("ones", [P, P])
        wmax = sb("wmax", [P, 8])
        wrow = sb("wrow", [P, 4])
        sig = sb("sig", [P, 1])
        inv_sig = sb("inv_sig", [P, 1])
        bu_sig = sb("bu_sig", [P, KC])
        a_par = sb("a_par", [P, KC])
        cb_par = sb("cb_par", [P, KC])
        f_sc = sb("f_sc", [P, FC])
        f_inv = sb("f_inv", [P, FC])
        asum = sb("asum", [P, NCH])
        thr = sb("thr", [P, 4])
        thr_s = sb("thr_s", [P, 2])

        misc = [ctx.enter_context(nc.psum_tensor(f"misc{i}", [P, 512], F32)) for i in range(2)]
        f1b = [ctx.enter_context(nc.psum_tensor(f"f1b{i}", [P, 512], F32)) for i in range(2)]
        f2b = [ctx.enter_context(nc.psum_tensor(f"f2b{i}", [P, 512], F32)) for i in range(NB)]

        x_in = [sem(f"x_in{i}") for i in range(X_SLOTS)]
        par_in, wout_in, row_in = sem("par_in"), sem("wout_in"), sem("row_in")
        win_in = [sem(f"win_in{k}") for k in range(KC)]
        chunk_in = [sem(f"chunk_in{i}") for i in range(W_SLOTS)]
        out_st = [sem(f"out_st{i}") for i in range(NB)]
        const_ok, prep, pmx, pm1 = sem("const_ok"), sem("prep"), sem("pmx"), sem("pm1")
        win_h, win_l, wo_h, wo_l = sem("win_h"), sem("win_l"), sem("wo_h"), sem("wo_l")
        abs_ok = [sem("abs_ok_act"), sem("abs_ok_dve")]
        thr_ok, thr_mm, t_ok, t2_ok, w_ok, w2_ok = (
            sem("thr_ok"), sem("thr_mm"), sem("t_ok"), sem("t2_ok"), sem("w_ok"), sem("w2_ok"))
        a_ok, tanh_ok = sem("a_ok"), sem("tanh_ok")
        bn_ok = [sem(f"bn_ok{i}") for i in range(5)]
        mv_ok = [sem(f"mv_ok{i}") for i in range(5)]
        ve_ok, pool_ok = sem("ve_ok"), sem("pool_ok")
        rs_ok = [sem(f"rs_ok{i}") for i in range(5)]
        xn_ok, t1_mm, x1_hi, x1_lo, v_mm, v_ok = (
            sem("xn_ok"), sem("t1_mm"), sem("x1_hi"), sem("x1_lo"), sem("v_mm"), sem("v_ok"))
        left_ok, right_ok = sem("left_ok"), sem("right_ok")
        tap1, tap0, tap2, scan_ok, carry_ok, dv_ok, y_ok, sy_ok, u_mm, g_ok, ghi_ok, glo_ok = (
            sem("tap1"), sem("tap0"), sem("tap2"), sem("scan_ok"), sem("carry_ok"), sem("dv_ok"),
            sem("y_ok"), sem("sy_ok"), sem("u_mm"), sem("g_ok"), sem("ghi_ok"), sem("glo_ok"))
        res_ok, resb_ok, o_mm, h_ok, a1_ok, a2_ok, x1_ok, n3_ok, t3_mm, x3_hi, x3_lo = (
            sem("res_ok"), sem("resb_ok"), sem("o_mm"), sem("h_ok"), sem("a1_ok"), sem("a2_ok"),
            sem("x1_ok"), sem("n3_ok"), sem("t3_mm"), sem("x3_hi"), sem("x3_lo"))
        f2_sum, fin_last = sem("f2_sum"), sem("fin_last")
        f1_mm, gelu_ok, hh_ok, hl_ok, f2_mm, f_ok, fn_ok, fin_ok = (
            sem("f1_mm"), sem("gelu_ok"), sem("hh_ok"), sem("hl_ok"), sem("f2_mm"), sem("f_ok"),
            sem("fn_ok"), sem("fin_ok"))

        def tiles(s):
            return [t if 0 <= t < NT else None for t in (s - 2, s - 1, s + 1, s - 3)]

        groups = []
        for s in STEPS:
            fa, c, n, _ = tiles(s)
            if c is not None:
                groups += [("u", c, b) for b in range(KC)]
            if n is not None:
                groups += [("t1", n, j) for j in range(NB)] + [("v", n, 0)]
            if c is not None:
                groups += [("o", c, j) for j in range(NB)]
            if n is not None:
                groups += [("v", n, b) for b in range(1, KC)]
            if c is not None:
                groups += [("t3", c, j) for j in range(NB)]
        misc_no = {g: i for i, g in enumerate(groups)}
        reader = {"u": g_ok, "t1": x1_lo, "v": v_ok, "o": h_ok, "t3": x3_lo}

        def bank(kind, t, i):
            return misc[misc_no[kind, t, i] % 2]

        def mean_var(ln):
            return mv[:, ln, :, :]

        def raw_stats(ln):
            return bn[:, ln, :, :]

        block = ctx.enter_context(nc.Block())

        @block.sync
        def _(sp):
            def load_x(t):
                if t >= X_SLOTS:
                    sp.wait_ge(fin_ok, NB * (t - X_SLOTS + 1))
                if t == X_SLOTS - 1:
                    sp.wait_ge(w_ok, NCH)
                sp.dma_start(xs[:, t % X_SLOTS, :, :], x_d[t]).then_inc(x_in[t % X_SLOTS], 16)

            def load_chunk(i):
                if i >= W_SLOTS:
                    sp.wait_ge(abs_ok[i % 2], min((i - W_SLOTS) // 2 + 1, NCH // 2))
                if i - W_SLOTS >= NCH:
                    sp.wait_ge(w_ok, i - W_SLOTS - NCH + 1)
                sp.dma_start(wch[:, i % W_SLOTS, :], chunks[i % NCH]).then_inc(chunk_in[i % W_SLOTS], 16)

            def store(t, j):
                if t < NT - 1:
                    sp.wait_ge(fin_ok, NB * t + j + 1)
                else:
                    sp.wait_ge(fin_last, j + 1)
                sp.dma_start(out_d[t, j], hb[:, j, :]).then_inc(out_st[j], 16)

            load_x(0)
            for k in range(KC):
                sp.dma_start(wf[:, k, :], w_in_d[:, k, :]).then_inc(win_in[k], 16)
            sp.dma_start(par[:, :], params).then_inc(par_in, 16)
            load_x(1)
            sp.dma_start(yb[:, :, :], w_out_d).then_inc(wout_in, 16)
            for i in range(NCH):
                load_chunk(i)
            load_x(2)
            sp.dma_start(row[:, :, :], rows.partition_broadcast(P)).then_inc(row_in, 16)
            for i in range(NCH, 2 * NCH):
                load_chunk(i)
            load_x(3)
            for s in STEPS:
                _, _, _, e = tiles(s)
                if e is not None:
                    for j in range(NB):
                        store(e, j)
                    if e + X_SLOTS < NT:
                        load_x(e + X_SLOTS)
            for j in range(NB):
                store(NT - 1, j)
            for j in range(NB):
                sp.wait_ge(out_st[j], 16 * NT)

        @block.tensor
        def _(pe):
            def take(kind, t, i):
                m = misc_no[kind, t, i]
                if m >= 2:
                    k, t0, i0 = groups[m - 2]
                    pe.wait_ge(reader[k], 4 * t0 + i0 + 1)
                return bank(kind, t, i)

            def transposes(kind, t, j, src, done):
                b = take(kind, t, j)
                for k in range(KC):
                    mm = pe.transpose(b[:, k * P:(k + 1) * P], src[:, k * P:(k + 1) * P], ident[:, :])
                mm.then_inc(done, 1)

            def t1(n, j):
                pe.wait_ge(xn_ok, NB * n + j + 1)
                transposes("t1", n, j, xn[:, j % 2, :], t1_mm)

            def t3(c, j):
                pe.wait_ge(n3_ok, NB * c + j + 1)
                transposes("t3", c, j, hb[:, j, :], t3_mm)

            def in_proj(kind, t, b, done):
                pe.wait_ge(x1_lo, NB * (t + 1))
                o = take(kind, t, b)
                c0_, s_ = (D if kind == "v" else 0) + b * P, t % 2
                for k in range(KC):
                    wh, wl = win_hi[:, k, c0_:c0_ + P], win_lo[:, k, c0_:c0_ + P]
                    pe.matmul(o[:, :], wh, x1T_hi[:, s_, k, :], start=k == 0, stop=False)
                    pe.matmul(o[:, :], wh, x1T_lo[:, s_, k, :], start=False, stop=False)
                    mm = pe.matmul(o[:, :], wl, x1T_hi[:, s_, k, :], start=False, stop=k == KC - 1)
                mm.then_inc(done, 1)

            def o(c, j):
                out_ = take("o", c, j)
                js = slice(j * P, (j + 1) * P)
                for k in range(KC):
                    pe.wait_ge(glo_ok, KC * c + k + 1)
                    pe.matmul(out_[:, :], g_hi[:, k, js], wo_hi[:, k, :], start=k == 0, stop=False)
                    pe.matmul(out_[:, :], g_hi[:, k, js], wo_lo[:, k, :], start=False, stop=False)
                    mm = pe.matmul(out_[:, :], g_lo[:, k, js], wo_hi[:, k, :], start=False, stop=k == KC - 1)
                mm.then_inc(o_mm, 1)

            def f1(t, j):
                i = FC * t + j
                if j == 0:
                    pe.wait_ge(x3_lo, NB * (t + 1))
                if i >= 2:
                    pe.wait_ge(gelu_ok, i - 1)
                b = f1b[i % 2]
                for k in range(KC):
                    w = w1[:, k, j * P:(j + 1) * P]
                    pe.matmul(b[:, :], w, x3T_hi[:, k, :], start=k == 0, stop=False)
                    mm = pe.matmul(b[:, :], w, x3T_lo[:, k, :], start=False, stop=k == KC - 1)
                mm.then_inc(f1_mm, 1)

            def f2_last():
                pe.wait_ge(hl_ok, FC * NT)
                for q in range(NB):
                    for j in range(FC - LAG, FC):
                        i, qs = FC * (NT - 1) + j, slice(q * P, (q + 1) * P)
                        pe.matmul(f2b[q][:, :], h_hi[:, i % H_SLOTS, qs], w2[:, j, :], start=False, stop=False)
                        mm = pe.matmul(f2b[q][:, :], h_lo[:, i % H_SLOTS, qs], w2[:, j, :], start=False, stop=j == FC - 1)
                    mm.then_inc(f2_sum, 1)

            def f2(t, j):
                i = FC * t + j
                if j == 0 and t > 0:
                    pe.wait_ge(f_ok, NB * t)
                pe.wait_ge(hl_ok, i + 1)
                if t == 0:
                    pe.wait_ge(w2_ok, j + 1)
                for q in range(NB):
                    qs = slice(q * P, (q + 1) * P)
                    pe.matmul(f2b[q][:, :], h_hi[:, i % H_SLOTS, qs], w2[:, j, :], start=j == 0, stop=False)
                    mm = pe.matmul(f2b[q][:, :], h_lo[:, i % H_SLOTS, qs], w2[:, j, :], start=False, stop=j == FC - 1)
                mm.then_inc(f2_mm, 1)

            def setup_in_proj():
                pe.wait_ge(pmx, KC + 1)
                pe.transpose(f2b[0][0:1, 0:P], wmax[:, 5:6], ident[:, :]).then_inc(pm1, 1)
                pe.wait_ge(pmx, KC + 2)
                pe.matmul(f2b[1][:, 0:1], ones[0:1, :], wrow[0:1, 0:1], start=True, stop=True).then_inc(pm1, 1)

            pe.wait_ge(const_ok, 3)
            for s in STEPS:
                fa, c, n, _ = tiles(s)
                if fa is not None:
                    if fa == 0:
                        pe.wait_ge(w_ok, NCH // 2)
                    for j in range(HALF):
                        f1(fa, j)
                        if j >= LAG:
                            f2(fa, j - LAG)
                if s == 1:
                    pe.wait_ge(thr_ok, 1)
                    pe.matmul(f2b[2][:, 0:2], ones[:, :], thr_s[:, :], start=True, stop=True).then_inc(thr_mm, 1)
                left = [lambda j=j: f2(fa, j) for j in range(HALF - LAG, HALF)] if fa is not None else 3 * [lambda: None]
                if c is not None:
                    if c == 0:
                        pe.wait_ge(win_l, 2 * KC)
                    for b in range(KC):
                        in_proj("u", c, b, u_mm)
                if n is not None:
                    t1(n, 0)
                    left[0]()
                    t1(n, 1)
                    left[1]()
                    if n == 0:
                        setup_in_proj()
                    t1(n, 2)
                    t1(n, 3)
                    left[2]()
                    if n == 0:
                        pe.wait_ge(win_l, KC)
                    in_proj("v", n, 0, v_mm)
                else:
                    for f in left:
                        f()
                if c is not None:
                    if c == 0:
                        pe.wait_ge(wo_l, KC)
                    for j in range(NB):
                        o(c, j)
                if n is not None:
                    for b in range(1, KC):
                        in_proj("v", n, b, v_mm)
                if fa is not None:
                    for j in range(HALF, FC):
                        f1(fa, j)
                        if j >= HALF + LAG:
                            f2(fa, j - LAG)
                left = [lambda j=j: f2(fa, j) for j in range(FC - LAG, FC)] if fa is not None else 3 * [lambda: None]
                if fa == NT - 1:
                    left = [f2_last] + 2 * [lambda: None]
                left[0]()
                if c is not None:
                    t3(c, 0)
                    t3(c, 1)
                left[1]()
                if c is not None:
                    t3(c, 2)
                    t3(c, 3)
                left[2]()

        @block.vector
        def _(ve_):
            chain = [0]

            def link(ins):
                ins.then_inc(prep, 1)
                chain[0] += 1
                ve_.wait_ge(prep, chain[0])

            def stats(ln, t, j, src):
                if t > 0:
                    ve_.wait_ge(mv_ok[ln], NB * (t - 1) + j + 1)
                ve_.bn_stats(raw_stats(ln)[:, j, :], src).then_inc(bn_ok[ln], 1)

            def aggr(ln, t, j):
                ve_.wait_ge(bn_ok[ln], NB * t + j + 1)
                if t > 0:
                    ve_.wait_ge(rs_ok[ln], t)
                ve_.bn_aggr(mean_var(ln)[:, j, :], raw_stats(ln)[:, j, :]).then_inc(mv_ok[ln], 1)

            def lo(t, j):
                i = FC * t + j
                ve_.wait_ge(hh_ok, i + 1)
                ve_.scalar_tensor_tensor(out=h_lo[:, i % H_SLOTS, :], in0=gg[:, i % G_SLOTS, :],
                                         scalar=f_sc[:, j:j + 1], in1=h_hi[:, i % H_SLOTS, :],
                                         op0=ALU.mult, op1=ALU.subtract).then_inc(hl_ok, 1)

            def f_add(e, j):
                if e == NT - 1:
                    ve_.wait_ge(f2_sum, j + 1)
                elif j == 0:
                    ve_.wait_ge(f2_mm, FC * (e + 1))
                if e + 1 < NT:
                    ve_.wait_ge(t3_mm, NB * (e + 1) + j + 1)
                else:
                    ve_.wait_ge(out_st[j], 16 * e)
                ve_.tensor_tensor(hb[:, j, :], f2b[j][:, :], b2_row, ALU.add).then_inc(f_ok, 1)

            def f_stats(e, j):
                ve_.wait_ge(f_ok, NB * e + j + 1)
                stats(4, e, j, hb[:, j, :])

            def epilogue(e):
                return (spread(AT_F_ADD, .2, [lambda j=j: f_add(e, j) for j in range(NB)])
                        + spread(AT_F_STATS, .2, [lambda j=j: f_stats(e, j) for j in range(NB)])
                        + spread(AT_F_AGGR, .05, [lambda j=j: aggr(4, e, j) for j in range(NB)]))

            def ln1(n, at=AT_LN1):
                def st(j):
                    if j == 0:
                        ve_.wait_ge(x_in[n % X_SLOTS], 16 * (n // X_SLOTS + 1))
                    stats(0, n, j, xs[:, n % X_SLOTS, j, :])
                return (spread(at, .01, [lambda j=j: st(j) for j in range(NB)])
                        + spread(at + .04, .001, [lambda j=j: aggr(0, n, j) for j in range(NB)]))

            def conv_scan(c):
                def taps(b, first):
                    i = KC * c + b
                    if first:
                        ve_.wait_ge(tap1, i + 1)
                        if b == 0:
                            ve_.wait_ge(left_ok, c + 1)
                            ve_.wait_ge(right_ok, c + 1)
                        src, w, done = v[:, c % 2, b, 0:TT], par[:, CW + b:CW + b + 1], tap0
                    else:
                        ve_.wait_ge(tap0, i + 1)
                        src, w, done = v[:, c % 2, b, 2:TT + 2], par[:, CW + 8 + b:CW + 9 + b], tap2
                    dst = vl[:, i % 2, :]
                    ve_.scalar_tensor_tensor(out=dst, in0=src, scalar=w, in1=dst,
                                             op0=ALU.mult, op1=ALU.add).then_inc(done, 1)

                def scan(b):
                    i = KC * c + b
                    ve_.wait_ge(tap2, i + 1)
                    if i >= 2:
                        ve_.wait_ge(y_ok, i - 1)
                        ve_.wait_ge(carry_ok, i - 1)
                    if c > 0:
                        ve_.wait_ge(carry_ok, i - KC + 1)
                    ve_.tensor_tensor_scan(out=ss[:, i % 2, :], data0=a_par[:, b:b + 1].to_broadcast([P, TT]),
                                           data1=vl[:, i % 2, :],
                                           initial=carry[:, b:b + 1] if c > 0 else 0.0,
                                           op0=ALU.mult, op1=ALU.add).then_inc(scan_ok, 1)

                def y(b):
                    i = KC * c + b
                    ve_.wait_ge(scan_ok, i + 1)
                    ve_.wait_ge(dv_ok, i + 1)
                    dst = yb[:, b, :]
                    ve_.scalar_tensor_tensor(out=dst, in0=ss[:, i % 2, :], scalar=cb_par[:, b:b + 1], in1=dst,
                                             op0=ALU.mult, op1=ALU.add).then_inc(y_ok, 1)

                items = []
                for b, at in zip(range(0, KC, 2), AT_PAIR):
                    items += spread(at, .2, [lambda b=b: taps(b, True), lambda b=b: taps(b + 1, True),
                                             lambda b=b: taps(b, False), lambda b=b: taps(b + 1, False)])
                    items += spread(at + .9, .4, [lambda b=b: scan(b), lambda b=b: scan(b + 1)])
                    items += spread(at + 1.8, .2, [lambda b=b: y(b), lambda b=b: y(b + 1)])
                return items

            def gate(c, b):
                i = KC * c + b
                ve_.wait_ge(sy_ok, i + 1)
                ve_.wait_ge(u_mm, i + 1)
                dst = yb[:, b, :]
                ve_.scalar_tensor_tensor(out=dst, in0=bank("u", c, b)[:, :], scalar=bu_sig[:, b:b + 1], in1=dst,
                                         op0=ALU.add, op1=ALU.mult).then_inc(g_ok, 1)

            def gate_lo(c, b):
                ve_.wait_ge(ghi_ok, KC * c + b + 1)
                ve_.tensor_tensor(g_lo[:, b, :], yb[:, b, :], g_hi[:, b, :].bitcast(F32),
                                  ALU.subtract).then_inc(glo_ok, 1)

            def t_lo(kind, t, j):
                hi, lo_, ok, done = ((x1T_hi[:, t % 2], x1T_lo[:, t % 2], x1_hi, x1_lo) if kind == "t1"
                                     else (x3T_hi, x3T_lo, x3_hi, x3_lo))
                ve_.wait_ge(ok, NB * t + j + 1)
                js = slice(j * P, (j + 1) * P)
                ve_.scalar_tensor_tensor(out=lo_[:, :, js], in0=bank(kind, t, j)[:, :].rearrange("p (k t) -> p k t", k=KC),
                                         scalar=ACT_SCALE, in1=hi[:, :, js],
                                         op0=ALU.mult, op1=ALU.subtract).then_inc(done, 1)

            def h_add(c, j):
                ve_.wait_ge(o_mm, NB * c + j + 1)
                ve_.wait_ge(resb_ok, NB * c + j + 1)
                ve_.scalar_tensor_tensor(out=hb[:, j, :], in0=bank("o", c, j)[:, :], scalar=inv_sig[:, 0:1],
                                         in1=hb[:, j, :], op0=ALU.mult, op1=ALU.add).then_inc(h_ok, 1)

            def h_stats(c, j):
                ve_.wait_ge(h_ok, NB * c + j + 1)
                stats(1, c, j, hb[:, j, :])

            def norms(c):
                xsl = xs[:, c % X_SLOTS]

                def a1(j):
                    if j == 0:
                        ve_.wait_ge(rs_ok[1], c + 1)
                    ve_.scalar_tensor_tensor(out=hb[:, j, :], in0=hb[:, j, :], scalar=mean_var(1)[:, j, 0:1],
                                             in1=lnw_row, op0=ALU.subtract, op1=ALU.mult).then_inc(a1_ok, 1)

                def a2(j):
                    ve_.wait_ge(a1_ok, NB * c + j + 1)
                    ve_.scalar_tensor_tensor(out=hb[:, j, :], in0=hb[:, j, :], scalar=rsc[:, 0, j:j + 1],
                                             in1=lnb_row, op0=ALU.mult, op1=ALU.add).then_inc(a2_ok, 1)

                def b_stats(j):
                    ve_.wait_ge(a2_ok, NB * c + j + 1)
                    stats(2, c, j, hb[:, j, :])

                def x1(j):
                    if j == 0:
                        ve_.wait_ge(rs_ok[2], c + 1)
                    ve_.scalar_tensor_tensor(out=xsl[:, j, :], in0=hb[:, j, :], scalar=rsc[:, 1, j:j + 1],
                                             in1=xsl[:, j, :], op0=ALU.mult, op1=ALU.add).then_inc(x1_ok, 1)

                def c_stats(j):
                    ve_.wait_ge(x1_ok, NB * c + j + 1)
                    stats(3, c, j, xsl[:, j, :])

                def n3(j):
                    if j == 0:
                        ve_.wait_ge(rs_ok[3], c + 1)
                    ve_.tensor_scalar(hb[:, j, :], xsl[:, j, :], mean_var(3)[:, j, 0:1], rsc[:, 2, j:j + 1],
                                      ALU.subtract, ALU.mult).then_inc(n3_ok, 1)

                kinds = [a1, a2, b_stats, lambda j: aggr(2, c, j), x1, c_stats, lambda j: aggr(3, c, j), n3]
                return spread(AT_NORMS, .2, [lambda f=f, j=j: f(j) for f in kinds for j in range(NB)])

            def setup_in_proj():
                for k in range(KC):
                    ve_.wait_ge(win_in[k], 16)
                    ve_.tensor_reduce(wmax[:, k:k + 1], wf[:, k, :], AX.X, ALU.max,
                                      apply_absolute_value=True).then_inc(pmx, 1)
                ve_.wait_ge(pmx, KC)
                link(ve_.tensor_reduce(wmax[:, 4:5], wmax[:, 0:KC], AX.X, ALU.max))
                ve_.tensor_scalar(wmax[:, 5:6].bitcast(U32), wmax[:, 4:5].bitcast(U32), 0x7F800000, None,
                                  ALU.bitwise_and).then_inc(pmx, 1)
                ve_.wait_ge(pm1, 1)
                ve_.tensor_reduce(wrow[0:1, 0:1], f2b[0][0:1, 0:P], AX.X, ALU.max).then_inc(pmx, 1)
                ve_.wait_ge(pm1, 2)
                ve_.tensor_scalar(wmax[:, 6:7], f2b[1][:, 0:1], 2.0 ** -100, 2.0 ** -13,
                                  ALU.max, ALU.mult).then_inc(pmx, 1)
                ve_.wait_ge(pmx, KC + 3)
                link(ve_.reciprocal(wmax[:, 7:8], wmax[:, 6:7]))
                link(ve_.tensor_scalar(inv_sig[:, :], wmax[:, 6:7], 1.0 / ACT_SCALE, None, ALU.mult))
                link(ve_.tensor_scalar(sig[:, :], wmax[:, 7:8], ACT_SCALE, None, ALU.mult))

            def setup_split():
                for i in range(2 * KC):
                    k, hs = i % KC, (D if i < KC else 0)
                    ve_.wait_ge(win_h, i + 1)
                    ve_.scalar_tensor_tensor(out=win_lo[:, k, hs:hs + D], in0=wf[:, k, hs:hs + D],
                                             scalar=wmax[:, 7:8], in1=win_hi[:, k, hs:hs + D],
                                             op0=ALU.mult, op1=ALU.subtract).then_inc(win_l, 1)

            def setup_params():
                ve_.wait_ge(par_in, 16)
                link(ve_.tensor_scalar(bu_sig[:, :], par[:, BIN:BIN + KC], sig[:, 0:1], None, ALU.mult))
                link(ve_.tensor_tensor(cb_par[:, :], par[:, SC:SC + KC], par[:, SB:SB + KC], ALU.mult))
                ve_.wait_ge(tanh_ok, 1)
                ve_.tensor_scalar(a_par[:, :], a_par[:, :], 1.0, 0.5, ALU.add, ALU.mult).then_inc(a_ok, 1)
                ve_.wait_ge(a_ok, 1)
                link(ve_.tensor_scalar(f_inv[:, :].bitcast(U32), par[:, B1:B1 + FC].bitcast(U32), 0x7FFFFFFF, None,
                                       ALU.bitwise_and))
                link(ve_.tensor_scalar(f_sc[:, :], f_inv[:, :], 512.0, None, ALU.add))
                link(ve_.tensor_scalar(f_inv[:, :].bitcast(U32), f_sc[:, :].bitcast(U32), 0x7F800000, None,
                                       ALU.bitwise_and))
                link(ve_.tensor_scalar(f_inv[:, :], f_inv[:, :], 2.0 ** -14, None, ALU.mult))
                link(ve_.reciprocal(f_sc[:, :], f_inv[:, :]))

            def setup_out_proj(k):
                ve_.wait_ge(wo_h, k + 1)
                ve_.tensor_tensor(wo_lo[:, k, :], yb[:, k, :], wo_hi[:, k, :].bitcast(F32),
                                  ALU.subtract).then_inc(wo_l, 1)

            def setup_thresholds():
                ve_.wait_ge(abs_ok[0], NCH // 2)
                ve_.wait_ge(abs_ok[1], NCH // 2)
                link(ve_.tensor_reduce(thr_s[:, 0:1], asum[:, 0:NCH // 2], AX.X, ALU.add))
                ve_.tensor_reduce(thr_s[:, 1:2], asum[:, NCH // 2:NCH], AX.X, ALU.add).then_inc(thr_ok, 1)
                ve_.wait_ge(thr_mm, 1)
                link(ve_.tensor_scalar(thr[:, 0:2], f2b[2][:, 0:2], 1.0 / (D * FF), 1e-8, ALU.mult, ALU.max))
                link(ve_.tensor_scalar(thr[:, 0:2], thr[:, 0:2], 0.5, None, ALU.mult))
                ve_.tensor_scalar(thr[:, 2:4], thr[:, 0:2], -1.0, None, ALU.mult).then_inc(thr_ok, 1)
                ve_.wait_ge(thr_ok, 2)

            def abs_sum(i):
                ve_.wait_ge(chunk_in[i % W_SLOTS], 16 * (i // W_SLOTS + 1))
                ve_.tensor_reduce(asum[:, i:i + 1], wch[:, i % W_SLOTS, :], AX.X, ALU.add,
                                  apply_absolute_value=True).then_inc(abs_ok[1], 1)

            def ternary(i, first):
                m, q = i // (NCH // 2), NCH + i
                src = wch[:, q % W_SLOTS, :]
                dst = w1[:, i // NQ, (i % NQ) * 512:(i % NQ) * 512 + 512] if m == 0 else w2[:, i - NCH // 2, :]
                if first:
                    ve_.wait_ge(chunk_in[q % W_SLOTS], 16 * (q // W_SLOTS + 1))
                    ve_.tensor_scalar(dst, src, thr[:, 2 + m:3 + m], 1.0, ALU.is_ge, ALU.subtract).then_inc(t_ok, 1)
                else:
                    if m == 0:
                        ve_.wait_ge(t_ok, i + 1)
                    else:
                        ve_.wait_ge(t2_ok, i - NCH // 2 + 1)
                    ve_.scalar_tensor_tensor(out=dst, in0=src, scalar=thr[:, m:m + 1], in1=dst,
                                             op0=ALU.is_gt, op1=ALU.add).then_inc(w_ok, 1)

            def convert(at, step, part):
                return (spread(at, step, [lambda i=i: ternary(i, True) for i in part])
                        + spread(at + 1.1 * step, step, [lambda i=i: ternary(i, False) for i in part]))

            run(ln1(0))
            setup_in_proj()
            for s in STEPS:
                fa, c, n, e = tiles(s)
                items = []
                if e is not None:
                    items += epilogue(e)
                if n is not None and s not in (-1, 0, 1):
                    items += ln1(n)
                if c is not None:
                    items += conv_scan(c)
                if s == 1:
                    for b, at in zip(range(0, KC, 2), AT_PAIR):
                        items += spread(at + 2.1, .1, [lambda b=b: gate(c, b), lambda b=b: gate(c, b + 1),
                                                       lambda b=b: gate_lo(c, b), lambda b=b: gate_lo(c, b + 1)])
                if fa is not None:
                    items += spread(1.2, 1, [lambda j=j: lo(fa, j) for j in range(HALF)])
                if s == 1:
                    items += ln1(2, AT_PAIR[1] + 2.05)
                    items.append((0, setup_thresholds))
                    items += convert(.1, .1, range(6))
                if s == 2:
                    items += [(at_w2(j) + .8, lambda j=j: ternary(NCH // 2 + j, False)) for j in range(FC)]
                run(items)
                if c is not None and c > 0:
                    gate(c, 0)
                    for b in range(1, KC):
                        gate(c, b)
                        gate_lo(c, b - 1)
                if n is not None:
                    t_lo("t1", n, 0)
                if c is not None and c > 0:
                    gate_lo(c, KC - 1)
                if n is not None:
                    for j in range(1, NB):
                        t_lo("t1", n, j)
                if s == -1:
                    setup_split()
                    setup_params()
                    run(ln1(1))
                if s < 1:
                    for i in range(1, NCH // 2, 2):
                        abs_sum(NCH // 2 * (s + 1) + i)
                if s == 0:
                    for k in range(KC):
                        setup_out_proj(k)
                items = []
                if s == 1:
                    run(convert(0, 1, range(6, NCH // 2 - 4)))
                if c is not None:
                    for j in range(NB):
                        if s == 1:
                            run(convert(0, 1, [NCH // 2 - 4 + j]))
                        h_add(c, j)
                        if j:
                            h_stats(c, j - 1)
                            if j > 1:
                                aggr(1, c, j - 2)
                    h_stats(c, NB - 1)
                    aggr(1, c, NB - 2)
                    aggr(1, c, NB - 1)
                    items = norms(c)
                if fa is not None:
                    items += spread(HALF + 1.2, 1, [lambda j=j: lo(fa, j) for j in range(HALF, FC)])
                run(items)
                if c is not None:
                    for j in range(NB):
                        t_lo("t3", c, j)
            e = NT - 1
            for j in range(NB + 1):
                if j < NB:
                    f_add(e, j)
                    f_stats(e, j)
                    aggr(4, e, j)
                if j:
                    ve_.wait_ge(fn_ok, NB * e + j)
                    ve_.tensor_tensor(hb[:, j - 1, :], hb[:, j - 1, :], xs[:, e % X_SLOTS, j - 1, :],
                                      ALU.add).then_inc(fin_last, 1)

        @block.scalar
        def _(act):
            def gelu(t, j):
                i = FC * t + j
                act.wait_ge(f1_mm, i + 1)
                if i >= G_SLOTS:
                    act.wait_ge(hl_ok, i - G_SLOTS + 1)
                act.activation(gg[:, i % G_SLOTS, :], f1b[i % 2][:, :], ACT.Gelu,
                               bias=par[:, B1 + j:B1 + j + 1], scale=1.0 / ACT_SCALE).then_inc(gelu_ok, 1)

            def hi(t, j):
                i = FC * t + j
                act.wait_ge(gelu_ok, i + 1)
                if i >= H_SLOTS:
                    act.wait_ge(f2_mm, i - H_SLOTS + 1)
                else:
                    act.wait_ge(abs_ok[0], NCH // 2)
                act.activation(h_hi[:, i % H_SLOTS, :], gg[:, i % G_SLOTS, :], ACT.Copy,
                               scale=f_sc[:, j:j + 1]).then_inc(hh_ok, 1)

            def ffn(t, js):
                return (spread(js[0], 1, [lambda j=j: gelu(t, j) for j in js])
                        + spread(js[0] + 1.1, 1, [lambda j=j: hi(t, j) for j in js]))

            def ffn_norm(e, j):
                if j == 0:
                    act.wait_ge(rs_ok[4], e + 1)
                act.activation(hb[:, j, :], hb[:, j, :], ACT.Identity, bias=nm4[:, j:j + 1],
                               scale=rs4[:, j:j + 1]).then_inc(fn_ok, 1)

            def centre_tap(c, b):
                i = KC * c + b
                act.wait_ge(v_ok, i + 1)
                if i >= 2:
                    act.wait_ge(scan_ok, i - 1)
                    act.wait_ge(dv_ok, i - 1)
                act.activation(vl[:, i % 2, :], v[:, c % 2, b, 1:TT + 1], ACT.Identity,
                               bias=par[:, CB + b:CB + b + 1], scale=par[:, CW + 4 + b:CW + 5 + b]).then_inc(tap1, 1)

            def d_conv(c, b):
                i = KC * c + b
                act.wait_ge(tap2, i + 1)
                if c > 0:
                    act.wait_ge(glo_ok, i - KC + 1)
                elif b == 0:
                    act.wait_ge(wo_l, KC)
                act.activation(yb[:, b, :], vl[:, i % 2, :], ACT.Copy,
                               scale=par[:, SD + b:SD + b + 1]).then_inc(dv_ok, 1)

            def residual(c, j):
                if c > 0:
                    act.wait_ge(t3_mm, NB * (c - 1) + j + 1)
                if c > 1:
                    act.wait_ge(out_st[j], 16 * (c - 1))
                act.activation(hb[:, j, :], xs[:, c % X_SLOTS, j, :], ACT.Identity, bias=nm1[:, c % 4, j:j + 1],
                               scale=rs1[:, c % 4, j:j + 1]).then_inc(res_ok, 1)

            def silu_y(c, b):
                act.wait_ge(y_ok, KC * c + b + 1)
                act.activation(yb[:, b, :], yb[:, b, :], ACT.Silu).then_inc(sy_ok, 1)

            def gate_hi(c, b):
                act.wait_ge(g_ok, KC * c + b + 1)
                if b == 0 and c > 0:
                    act.wait_ge(o_mm, NB * c)
                act.activation(g_hi[:, b, :], yb[:, b, :], ACT.Copy).then_inc(ghi_ok, 1)

            def norm_x(n, j):
                i = NB * n + j
                if j == 0:
                    act.wait_ge(rs_ok[0], n + 1)
                if i >= 2:
                    act.wait_ge(t1_mm, i - 1)
                act.activation(xn[:, i % 2, :], xs[:, n % X_SLOTS, j, :], ACT.Identity, bias=nm1[:, n % 4, j:j + 1],
                               scale=rs1[:, n % 4, j:j + 1]).then_inc(xn_ok, 1)

            def t_hi(kind, t, j):
                if kind == "t1":
                    hi_, mm, done = x1T_hi[:, t % 2], t1_mm, x1_hi
                    if t > 1 and j == 0:
                        act.wait_ge(u_mm, KC * (t - 1))
                else:
                    hi_, mm, done = x3T_hi, t3_mm, x3_hi
                    if t > 0 and j == 0:
                        act.wait_ge(f1_mm, FC * t)
                act.wait_ge(mm, NB * t + j + 1)
                act.activation(hi_[:, :, j * P:(j + 1) * P], bank(kind, t, j)[:, :].rearrange("p (k t) -> p k t", k=KC),
                               ACT.Copy, scale=ACT_SCALE).then_inc(done, 1)

            def silu_v(n, b):
                act.wait_ge(v_mm, KC * n + b + 1)
                if n > 1 and b == 0:
                    act.wait_ge(tap2, KC * (n - 1))
                if n == 0 and b == 0:
                    act.wait_ge(win_l, 2 * KC)
                if n > 0 and b == 0:
                    act.wait_ge(left_ok, n)
                    if n > 1:
                        act.wait_ge(right_ok, n - 1)
                act.activation(v[:, n % 2, b, 1:TT + 1], bank("v", n, b)[:, :], ACT.Silu,
                               bias=par[:, BIN + KC + b:BIN + KC + b + 1], scale=inv_sig[:, 0:1]).then_inc(v_ok, 1)

            def abs_sum(i):
                act.wait_ge(chunk_in[i % W_SLOTS], 16 * (i // W_SLOTS + 1))
                n = i // 2
                if n >= H_SLOTS:
                    act.wait_ge(abs_ok[0], n - H_SLOTS + 1)
                act.activation(h_hi[:, n % H_SLOTS, :], wch[:, i % W_SLOTS, :], ACT.Abs,
                               accum_out=asum[:, i:i + 1]).then_inc(abs_ok[0], 1)

            def scale_w2(j):
                act.wait_ge(w_ok, NCH // 2 + j + 1)
                act.activation(w2[:, j, :], w2[:, j, :], ACT.Copy, scale=f_inv[:, j:j + 1]).then_inc(w2_ok, 1)

            act.wait_ge(par_in, 16)
            act.activation(a_par[:, :], par[:, LA:LA + KC], ACT.Tanh, scale=0.5).then_inc(tanh_ok, 1)
            for s in STEPS:
                fa, c, n, e = tiles(s)
                items = []
                if e is not None:
                    items += [(at, lambda j=j: ffn_norm(e, j)) for j, at in enumerate(AT_F_NORM)]
                if c is not None:
                    for b, at in zip(range(0, KC, 2), AT_PAIR):
                        items += spread(at - .3, .15, [lambda b=b: centre_tap(c, b), lambda b=b: centre_tap(c, b + 1)])
                        items += spread(at + 1.2, .4, [lambda b=b: d_conv(c, b), lambda b=b: d_conv(c, b + 1)])
                if fa is not None:
                    items += ffn(fa, range(HALF))
                if s == 1:
                    for b, at in zip(range(0, KC, 2), AT_PAIR):
                        items += spread(at + 2.05, .1, [lambda b=b: silu_y(c, b), lambda b=b: silu_y(c, b + 1),
                                                        lambda b=b: gate_hi(c, b), lambda b=b: gate_hi(c, b + 1)])
                if s == 2:
                    items += [(at_w2(j) + .9, lambda j=j: scale_w2(j)) for j in range(FC)]
                run(items)
                if c is not None and c > 0:
                    for b in range(KC):
                        silu_y(c, b)
                if n is not None and s != 0:
                    norm_x(n, 0)
                if c is not None and c > 0:
                    gate_hi(c, 0)
                if n is not None and s != 0:
                    norm_x(n, 1)
                if c is not None and c > 0:
                    gate_hi(c, 1)
                    gate_hi(c, 2)
                if n is not None:
                    t_hi("t1", n, 0)
                if c is not None and c > 0:
                    gate_hi(c, 3)
                if n is not None:
                    norm_x(n, 2)
                    t_hi("t1", n, 1)
                    norm_x(n, 3)
                    t_hi("t1", n, 2)
                    t_hi("t1", n, 3)
                if s == -1:
                    act.wait_ge(prep, 2)
                    for i in range(2 * KC):
                        k, hs = i % KC, (D if i < KC else 0)
                        act.activation(win_hi[:, k, hs:hs + D], wf[:, k, hs:hs + D], ACT.Copy,
                                       scale=wmax[:, 7:8]).then_inc(win_h, 1)
                if c is not None:
                    for j in range(NB // 2):
                        residual(c, j)
                if n is not None:
                    silu_v(n, 0)
                if c is not None:
                    for j in range(NB // 2, NB):
                        residual(c, j)
                if n is not None:
                    for b in range(KC):
                        if b:
                            silu_v(n, b)
                        if s == -1 and b > 1:
                            norm_x(1, b - 2)
                        if s < 1:
                            for i in range(0, NCH // 8, 2):
                                abs_sum((KC * (s + 1) + b) * NCH // 8 + i)
                if s == 0:
                    act.wait_ge(wout_in, 16)
                    for k in range(KC):
                        act.activation(wo_hi[:, k, :], yb[:, k, :], ACT.Copy).then_inc(wo_h, 1)
                if fa is not None:
                    run(ffn(fa, range(HALF, FC)))
                if c is not None:
                    for j in range(NB):
                        t_hi("t3", c, j)
            for j in range(NB):
                act.wait_ge(rs_ok[4], NT + j)
                ffn_norm(NT - 1, j)

        @block.gpsimd
        def _(pool):
            chain = [0]

            def link(ins):
                ins.then_inc(pool_ok, 1)
                chain[0] += 1
                pool.wait_ge(pool_ok, chain[0])

            def rstd(ln, t, dst, last, js=slice(0, NB)):
                pool.wait_ge(mv_ok[ln], NB * t + js.stop)
                link(pool.tensor_scalar(ve[:, ln, js], mean_var(ln)[:, js, 1], EPS, None, ALU.add))
                ins = pool.tensor_tensor(dst, ve[:, ln, js], mhalf[:, js], ALU.pow)
                if last:
                    ins.then_inc(rs_ok[ln], 1)
                else:
                    link(ins)

            def rstd_x(n):
                if n > 3:
                    pool.wait_ge(res_ok, NB * (n - 3))
                rstd(0, n, rs1[:, n % 4, :], False)
                link(pool.tensor_tensor(tmp4[:, 0, :], mean_var(0)[:, :, 0], rs1[:, n % 4, :], ALU.mult))
                pool.tensor_scalar(nm1[:, n % 4, :], tmp4[:, 0, :], -1.0, None, ALU.mult).then_inc(rs_ok[0], 1)

            def rstd_b(c):
                rstd(2, c, rsc[:, 1, :], False)
                pool.tensor_tensor(c0[:, c % 4, :], mean_var(2)[:, :, 0], rsc[:, 1, :], ALU.mult).then_inc(rs_ok[2], 1)

            def rstd_f(e, js=slice(0, NB)):
                if e > 0:
                    pool.wait_ge(fn_ok, NB * e)
                rstd(4, e, rs4[:, js], False, js)
                link(pool.tensor_tensor(tmp4[:, 1, js], mean_var(4)[:, js, 0], rs4[:, js], ALU.mult))
                link(pool.tensor_tensor(tmp4[:, 2, js], tmp4[:, 1, js], c0[:, e % 4, js], ALU.add))
                pool.tensor_scalar(nm4[:, js], tmp4[:, 2, js], -1.0, None, ALU.mult).then_inc(rs_ok[4], 1)

            def finish(e, j):
                pool.wait_ge(fn_ok, NB * e + j + 1)
                pool.tensor_tensor(hb[:, j, :], hb[:, j, :], xs[:, e % X_SLOTS, j, :], ALU.add).then_inc(fin_ok, 1)

            def keep_state(c, b):
                i = KC * c + b
                pool.wait_ge(scan_ok, i + 1)
                pool.tensor_copy(carry[:, b:b + 1], ss[:, i % 2, TT - 1:TT]).then_inc(carry_ok, 1)

            def add_bias(c, j):
                pool.wait_ge(res_ok, NB * c + j + 1)
                pool.tensor_tensor(hb[:, j, :], hb[:, j, :], ob_row, ALU.add).then_inc(resb_ok, 1)

            def edges(n):
                if n < NT:
                    pool.wait_ge(v_ok, KC * (n + 1))
                if n == 0:
                    pool.memset(v[:, 0, :, 0:1], 0.0).then_inc(left_ok, 1)
                    return
                if n < NT:
                    if n > 1:
                        pool.wait_ge(tap2, KC * (n - 1))
                    pool.tensor_copy(v[:, n % 2, :, 0:1], v[:, (n - 1) % 2, :, TT:TT + 1]).then_inc(left_ok, 1)
                    pool.tensor_copy(v[:, (n - 1) % 2, :, TT + 1:TT + 2], v[:, n % 2, :, 1:2]).then_inc(right_ok, 1)
                else:
                    pool.memset(v[:, (n - 1) % 2, :, TT + 1:TT + 2], 0.0).then_inc(right_ok, 1)

            def ternary_w2(j):
                q = NCH + NCH // 2 + j
                pool.wait_ge(chunk_in[q % W_SLOTS], 16 * (q // W_SLOTS + 1))
                pool.tensor_scalar(w2[:, j, :], wch[:, q % W_SLOTS, :], thr[:, 3:4], 1.0,
                                   ALU.is_ge, ALU.subtract).then_inc(t2_ok, 1)

            pool.memset(ident[:, :], 0.0).then_inc(const_ok, 1)
            pool.memset(ones[:, :], 1.0).then_inc(const_ok, 1)
            pool.wait_ge(const_ok, 2)
            pool.affine_select(out=ident[:, :], in_=ident[:, :], compare_op=ALU.not_equal, fill=1.0, base=0,
                               pattern=[[-1, P]], channel_multiplier=1).then_inc(const_ok, 1)
            link(pool.memset(mhalf[:, :], -0.5))
            for s in STEPS:
                fa, c, n, e = tiles(s)
                if e is not None:
                    rstd_f(e)
                    for j in range(NB):
                        finish(e, j)
                items = []
                if c is not None:
                    for b, at in zip(range(0, KC, 2), AT_PAIR):
                        items += spread(at + 1.0, .4, [lambda b=b: keep_state(c, b), lambda b=b: keep_state(c, b + 1)])
                if s == 2:
                    items += [(at_w2(j), lambda j=j: ternary_w2(j)) for j in range(W_SLOTS, FC)]
                run(items)
                if n is not None and s not in (-1, 0):
                    rstd_x(n)
                if s < 0:
                    rstd_x(0)
                    rstd_x(1)
                if c == 0:
                    pool.wait_ge(row_in, 16)
                if c is not None:
                    for j in range(NB):
                        add_bias(c, j)
                if s == 1:
                    pool.wait_ge(thr_ok, 2)
                    for j in range(W_SLOTS):
                        ternary_w2(j)
                if c is not None:
                    rstd(1, c, rsc[:, 0, :], True)
                    rstd_b(c)
                    rstd(3, c, rsc[:, 2, :], True)
                if n is not None:
                    edges(n)
                if s == NT - 1:
                    edges(NT)
            for j in range(NB):
                rstd_f(NT - 1, slice(j, j + 1))


def kernel(**inputs):
    import numpy as np
    import concourse.bacc as bacc
    from concourse.bass_utils import run_bass_kernel_spmd

    def get(name):
        return np.asarray(inputs[name])

    x = get("L0_attn_x")
    cols = [get("L0_attn_in_proj_b").reshape(-1, P)]
    cols += [get("L0_attn_conv_w")[:, 0, k].reshape(-1, P) for k in range(3)]
    cols += [get("L0_attn_" + n).reshape(-1, P) for n in ("conv_b", "logit_a", "ssm_b", "ssm_c", "ssm_d")]
    cols += [get("L0_ffn_b1").reshape(-1, P)]
    arrays = {
        "x_dram": x.reshape(-1, D),
        "w_in_dram": get("L0_attn_in_proj_w"),
        "w_out_dram": get("L0_attn_out_proj_w"),
        "w1t_dram": get("L0_ffn_W1").T,
        "w2t_dram": get("L0_ffn_W2").T,
        "params_dram": np.concatenate(cols, axis=0).T,
        "rows_dram": np.stack([get("L0_attn_out_proj_b"), get("L0_attn_ln_w"), get("L0_attn_ln_b"), get("L0_ffn_b2")]),
    }
    arrays = {n: np.ascontiguousarray(a) for n, a in arrays.items()}
    nc = bacc.Bacc("TRN2", target_bir_lowering=False, num_devices=1)
    args = [nc.dram_tensor(n, a.shape, mybir.dt.from_np(a.dtype), kind="ExternalInput").ap() for n, a in arrays.items()]
    out = nc.dram_tensor("out_dram", arrays["x_dram"].shape, F32, kind="ExternalOutput").ap()
    build(nc, *args, out)
    r = run_bass_kernel_spmd(nc, [arrays], core_ids=[0])
    return r.results[0]["out_dram"].reshape(x.shape)
```

```python
from contextlib import ExitStack

import concourse.bass as bass
from concourse import mybir

P = 128
D = 512
TT = 512
NB = TT // P
KC = D // P
LAG = 3
X_SLOTS = 4
G_SLOTS = 3
H_SLOTS = 4
T_SLOTS = 2
EPS = 1e-5
ACT_SCALE = 2048.0

F32 = mybir.dt.float32
F32R = mybir.dt.float32r
F16 = mybir.dt.float16
U32 = mybir.dt.uint32
ALU = mybir.AluOpType
ACT = mybir.ActivationFunctionType
AX = mybir.AxisListType

BIN, CW, CB, LA, SB, SC, SD, B1 = 0, 8, 20, 24, 28, 32, 36, 40
NPAR = 56
A_SLOTS = 2 * NB
W_SLOTS = NB


AT_F_ADD, AT_F_STATS, AT_F_AGGR = 0.0, 0.8, 1.6
AT_F_NORM = (2.7, 3.3, 4.4, 5.0)
AT_PAIR = (2.2, 5.0)
AT_LN1 = 9.0
AT_NORMS, AT_NORMS_END = 7.7, 6.7
AT_T3_HI = (15.2, 15.6, 17.1, 17.3)
AT_T3_LO = (15.3, 15.7, 17.15, 17.35)
AT_T3_HI_END, AT_T3_LO_END = (14.15, 14.4, 15.3, 16.2), (14.17, 14.19, 15.4, 16.25)
AT_V = (8.9, 8.95, 16.3, 17.2)
AT_V_2 = (16.2, 16.3, 17.2, 17.3)
AT_FRONT_2, AT_T_LO_2 = (10.5, 11.5, 12.5, 13.5), (10.6, 11.6, 12.6, 13.6)
W_PAIRS, W_OUT, W_NORMS = 8, 12, 15
W_GPSIMD = (0, 1, 2, 3, 4, 5, 7, 13, *range(W_NORMS, 28, 2))
AT_W_PAIRS = (5.7, 6.5, 7.46, 7.48, 7.6, 7.7, 7.8, 7.9)
AT_SCALE_LAST = (10.3, 10.6, 11.3, 11.6)
AT_FRONT = (7.5, 7.6, 7.7, 7.8)
AT_T_LO = (7.55, 7.65, 7.75, 7.85)
ABS_AFTER_V = {(0, 0): range(0, 3), (0, 2): range(3, 6),
               (1, -1): range(6, 12), (1, 0): range(12, 14), (1, 1): range(14, 16)}


def at_w(i):
    if i < W_PAIRS:
        return AT_PAIR[0] + 1.5 + .45 * i
    if i < W_NORMS:
        return AT_NORMS + (-.1, 3.9, 6.9)[i - W_OUT]
    return .62 * (i - W_NORMS)


def run(items):
    for _, work in sorted(items, key=lambda item: item[0]):
        work()


def spread(at, step, works):
    return [(at + step * i, w) for i, w in enumerate(works)]


def build(nc, x, w_in, w_out, w1t, w2t, params, rows, out):
    T = x.shape[0]
    NT = T // TT
    FF = w1t.shape[1]
    FC = FF // P

    def half(n):
        return (9 if n is not None else 7) * FC // 16

    STEPS = range(-1, NT + 2)

    x_d = x.rearrange("(t j p) d -> t p j d", p=P, j=NB)
    out_d = out.rearrange("(t j p) d -> t j p d", p=P, j=NB)
    w_in_d = w_in.rearrange("(k p) n -> p k n", p=P)
    w_out_d = w_out.rearrange("(k p) n -> p k n", p=P)
    w1_d = w1t.rearrange("(k p) (q n) -> q k p n", p=P, n=512)
    w2_d = w2t.rearrange("(c p) n -> c p n", p=P)
    NQ = FF // 512
    BQ = 512 // P
    chunks = [w1_d[i // KC, i % KC] for i in range(KC * NQ)] + [w2_d[c] for c in range(FC)]
    NCH = len(chunks)

    with ExitStack() as ctx:
        def sb(name, shape, dt=F32):
            return ctx.enter_context(nc.sbuf_tensor(name, shape, dt))

        def sem(name):
            return ctx.enter_context(nc.semaphore(name))

        win_hi = sb("win_hi", [P, KC, 2 * D], F16)
        win_lo = sb("win_lo", [P, KC, 2 * D], F16)
        wo_hi = sb("wo_hi", [P, KC, D], F32R)
        wo_lo = sb("wo_lo", [P, KC, D], F32R)
        w1 = sb("w1", [P, KC, FF], F16)
        w2 = sb("w2", [P, FC, D], F16)
        row = sb("row", [P, 4, D])
        ob_row, lnw_row, lnb_row, b2_row = (row[:, i, :] for i in range(4))
        ident = sb("ident", [P, P])
        par = sb("par", [P, NPAR])
        xs = sb("xs", [P, X_SLOTS, NB, D])
        xn = sb("xn", [P, D])
        tp = sb("tp", [P, T_SLOTS, 2, D], F16)
        hb = sb("hb", [P, NB, D])
        x1T = sb("x1T", [P, 2, 2 * KC, TT], F16)
        x3T = sb("x3T", [P, 2 * KC, TT], F16)
        vb = sb("vb", [P, 2 * KC * (TT + 2)])
        v = vb[:, :].rearrange("p (s k t) -> p s k t", s=2, k=KC)
        wf = vb[:, 0:KC * 2 * D].rearrange("p (k n) -> p k n", k=KC)
        vl = sb("vl", [P, 2, TT])
        ss = sb("ss", [P, 2, TT])
        yb = sb("yb", [P, KC, TT])
        g_hi = sb("g_hi", [P, KC, TT], F32R)
        g_lo = sb("g_lo", [P, KC, TT], F32R)
        gg = sb("gg", [P, G_SLOTS, TT])
        wch = xs[:, X_SLOTS - 2:, :, :].rearrange("p s j d -> p (s j) d")
        h_hi = sb("h_hi", [P, H_SLOTS, TT], F16)
        h_lo = sb("h_lo", [P, H_SLOTS, TT], F16)
        bn = sb("bn", [P, 5, NB, 6])
        mv = sb("mv", [P, 5, NB, 2])
        ve = sb("ve", [P, 5, NB])
        rs1 = sb("rs1", [P, 4, NB])
        nm1 = sb("nm1", [P, 4, NB])
        rsc = sb("rsc", [P, 3, NB])
        c0 = sb("c0", [P, 4, NB])
        rs4 = sb("rs4", [P, NB])
        nm4 = sb("nm4", [P, NB])
        mhalf = sb("mhalf", [P, NB])
        carry = sb("carry", [P, KC])
        tmp4 = sb("tmp4", [P, 3, NB])
        ones = sb("ones", [P, P])
        wmax = sb("wmax", [P, 8])
        wrow = sb("wrow", [P, 4])
        sig = sb("sig", [P, 1])
        inv_sig = sb("inv_sig", [P, 1])
        bu_sig = sb("bu_sig", [P, KC])
        a_par = sb("a_par", [P, KC])
        cb_par = sb("cb_par", [P, KC])
        f_sc = sb("f_sc", [P, FC])
        f_inv = sb("f_inv", [P, FC])
        asum = sb("asum", [P, NCH])
        thr = sb("thr", [P, 4])
        thr_s = sb("thr_s", [P, 2])

        misc = [ctx.enter_context(nc.psum_tensor(f"misc{i}", [P, 512], F32)) for i in range(2)]
        f1b = [ctx.enter_context(nc.psum_tensor(f"f1b{i}", [P, 512], F32)) for i in range(2)]
        f2b = [ctx.enter_context(nc.psum_tensor(f"f2b{i}", [P, 512], F32)) for i in range(NB)]

        x_in = [sem(f"x_in{i}") for i in range(X_SLOTS)]
        x0_in = [sem(f"x0_in{j}") for j in range(NB)]
        par_in, wout_in, row_in = sem("par_in"), sem("wout_in"), sem("row_in")
        win_in = [sem(f"win_in{k}") for k in range(KC)]
        chunk_in = [sem(f"chunk_in{i}") for i in range(A_SLOTS)]
        out_st = [sem(f"out_st{i}") for i in range(NB)]
        const_ok, prep, pmx, pm1 = sem("const_ok"), sem("prep"), sem("pmx"), sem("pm1")
        win_h, win_l, wo_h, wo_l = sem("win_h"), sem("win_l"), sem("wo_h"), sem("wo_l")
        abs_ok = [sem("abs_ok_act"), sem("abs_ok_dve")]
        thr_ok, thr_mm, tp_ok, td_ok, w_ok, w2_ok = (
            sem("thr_ok"), sem("thr_mm"), sem("tp_ok"), sem("td_ok"), sem("w_ok"), sem("w2_ok"))
        a_ok, tanh_ok = sem("a_ok"), sem("tanh_ok")
        bn_ok = [sem(f"bn_ok{i}") for i in range(5)]
        mv_ok = [sem(f"mv_ok{i}") for i in range(5)]
        ve_ok, pool_ok = sem("ve_ok"), sem("pool_ok")
        rs_ok = [sem(f"rs_ok{i}") for i in range(5)]
        xn_ok, x1_hi, x1_lo, v_mm, v_ok = sem("xn_ok"), sem("x1_hi"), sem("x1_lo"), sem("v_mm"), sem("v_ok")
        transposed = [sem(f"transposed{i}") for i in range(T_SLOTS)]
        left_ok, right_ok = sem("left_ok"), sem("right_ok")
        tap1, tap0, tap2, scan_ok, carry_ok, dv_ok, y_ok, sy_ok, u_mm, g_ok, ghi_ok, glo_ok = (
            sem("tap1"), sem("tap0"), sem("tap2"), sem("scan_ok"), sem("carry_ok"), sem("dv_ok"),
            sem("y_ok"), sem("sy_ok"), sem("u_mm"), sem("g_ok"), sem("ghi_ok"), sem("glo_ok"))
        res_ok, resb_ok, o_mm, h_ok, a1_ok, a2_ok, x1_ok, n3_ok, x3_hi, x3_lo = (
            sem("res_ok"), sem("resb_ok"), sem("o_mm"), sem("h_ok"), sem("a1_ok"), sem("a2_ok"),
            sem("x1_ok"), sem("n3_ok"), sem("x3_hi"), sem("x3_lo"))
        f2_sum, fin_last = sem("f2_sum"), sem("fin_last")
        f1_mm, gelu_ok, hh_ok, hl_ok, f2_mm, f_ok, fn_ok, fin_ok = (
            sem("f1_mm"), sem("gelu_ok"), sem("hh_ok"), sem("hl_ok"), sem("f2_mm"), sem("f_ok"),
            sem("fn_ok"), sem("fin_ok"))

        def tiles(s):
            return [t if 0 <= t < NT else None for t in (s - 2, s - 1, s + 1, s - 3)]

        groups = []
        for s in STEPS:
            _, c, n, _ = tiles(s)
            us = [("u", c, b) for b in range(KC)] if c is not None else []
            os_ = [("o", c, j) for j in range(NB)] if c is not None else []
            vs = [("v", n, b) for b in range(KC)] if n is not None else []
            if c == 0:
                us = []
            groups += us + os_ + vs
        misc_no = {g: i for i, g in enumerate(groups)}
        reader = {"u": g_ok, "v": v_ok, "o": h_ok}

        blocks = []
        for s in STEPS:
            _, c, n, _ = tiles(s)
            blocks += [("t1", n, j) for j in range(NB)] if n is not None else []
            blocks += [("t3", c, j) for j in range(NB)] if c is not None else []
        block_no = {b: i for i, b in enumerate(blocks)}

        def wait_transposed(eng, m):
            eng.wait_ge(transposed[m % T_SLOTS], 16 * (m // T_SLOTS + 1))

        def wait_tile(eng, kind, t):
            for j in range(NB - T_SLOTS, NB):
                wait_transposed(eng, block_no[kind, t, j])

        def bank(kind, t, i):
            if (kind, t) == ("u", 0):
                return f2b[i]
            return misc[misc_no[kind, t, i] % 2]

        def x3T_of(t):
            return x1T[:, t % 2] if t == NT - 2 else x3T

        def mean_var(ln):
            return mv[:, ln, :, :]

        def raw_stats(ln):
            return bn[:, ln, :, :]

        def sum_slot(i):
            return i % A_SLOTS, 16 * (i // A_SLOTS + 1)

        def conv_slot(i):
            return A_SLOTS - W_SLOTS + i % W_SLOTS, 16 * (NCH // A_SLOTS + i // W_SLOTS + 1)

        def chunk_dst(i):
            return w1[:, i % KC, (i // KC) * 512:(i // KC + 1) * 512] if i < NCH // 2 else w2[:, i - NCH // 2, :]

        def first_no(i):
            return len([q for q in range(i + 1) if (q in W_GPSIMD) == (i in W_GPSIMD)])

        def first_summand(eng, i, done):
            m, (slot, loaded) = i // (NCH // 2), conv_slot(i)
            eng.wait_ge(chunk_in[slot], loaded)
            eng.tensor_scalar(chunk_dst(i), wch[:, slot, :], thr[:, 2 + m:3 + m], 1.0,
                              ALU.is_ge, ALU.subtract).then_inc(done, 1)

        block = ctx.enter_context(nc.Block())

        @block.sync
        def _(sp):
            def load_x(t):
                if t >= X_SLOTS:
                    sp.wait_ge(fin_ok, NB * (t - X_SLOTS + 1))
                if t == X_SLOTS - 2:
                    sp.wait_ge(abs_ok[0], (NCH - W_SLOTS) // 2)
                    sp.wait_ge(abs_ok[1], (NCH - W_SLOTS) // 2)
                if t == X_SLOTS - 1:
                    sp.wait_ge(w_ok, NCH)
                sp.dma_start(xs[:, t % X_SLOTS, :, :], x_d[t]).then_inc(x_in[t % X_SLOTS], 16)

            def load_to_sum(i):
                if i >= A_SLOTS:
                    sp.wait_ge(abs_ok[i % 2], (i - A_SLOTS) // 2 + 1)
                slot, _ = sum_slot(i)
                sp.dma_start(wch[:, slot, :], chunks[i]).then_inc(chunk_in[slot], 16)

            def load_to_convert(i):
                if i < W_SLOTS:
                    sp.wait_ge(abs_ok[i % 2], (NCH - W_SLOTS + i) // 2 + 1)
                else:
                    sp.wait_ge(w_ok, i - W_SLOTS + 1)
                slot, _ = conv_slot(i)
                sp.dma_start(wch[:, slot, :], chunks[i]).then_inc(chunk_in[slot], 16)

            def store(t, j):
                if t < NT - 1:
                    sp.wait_ge(fin_ok, NB * t + j + 1)
                else:
                    sp.wait_ge(fin_last, j + 1)
                sp.dma_start(out_d[t, j], hb[:, j, :]).then_inc(out_st[j], 16)

            def transpose(kind, t, j):
                if kind == "t1":
                    dst, split = x1T[:, t % 2], x1_lo
                    if t > 1 and j == 0:
                        sp.wait_ge(u_mm, KC * (t - 1))
                else:
                    dst, split = x3T_of(t), x3_lo
                    if t == NT - 2 and j == 0:
                        sp.wait_ge(u_mm, KC * (t + 1))
                    elif t > 0 and j == 0:
                        sp.wait_ge(f1_mm, FC * min(t, NT - 2))
                r = block_no[kind, t, j] % T_SLOTS
                sp.wait_ge(split, NB * t + j + 1)
                sp.dma_start_transpose(dst[:, :, j * P:(j + 1) * P],
                                       tp[:, r].rearrange("p h d -> p (h d)")).then_inc(transposed[r], 16)

            def transposes(kind, t):
                for j in range(NB):
                    transpose(kind, t, j)

            sp.dma_start(par[:, :], params).then_inc(par_in, 16)
            for j in range(NB):
                sp.dma_start(xs[:, 0, j, :], x_d[0, :, j, :]).then_inc(x0_in[j], 16)
            for k in range(KC):
                sp.dma_start(wf[:, k, :], w_in_d[:, k, :]).then_inc(win_in[k], 16)
            load_x(1)
            for i in range(W_SLOTS):
                load_to_sum(i)
            transposes("t1", 0)
            for i in range(W_SLOTS, A_SLOTS):
                load_to_sum(i)
            sp.dma_start(yb[:, :, :], w_out_d).then_inc(wout_in, 16)
            for j, part in enumerate((range(8, 12), range(12, 14), range(14, 16), range(16, NCH))):
                transpose("t1", 1, j)
                for i in part:
                    load_to_sum(i)
            load_x(2)
            for i in range(W_SLOTS):
                load_to_convert(i)
            sp.dma_start(row[:, :, :], rows.partition_broadcast(P)).then_inc(row_in, 16)
            for i in range(W_SLOTS, 2 * W_SLOTS):
                load_to_convert(i)
            for j, i in enumerate(range(2 * W_SLOTS, 2 * W_SLOTS + NB)):
                transpose("t1", 2, j)
                load_to_convert(i)
            for i in range(2 * W_SLOTS + NB, W_SLOTS + W_NORMS):
                load_to_convert(i)
            transposes("t3", 0)
            for i in range(W_SLOTS + W_NORMS, NCH):
                load_to_convert(i)
            load_x(3)
            for s in range(2, NT + 2):
                _, c, n, e = tiles(s)
                if e is not None:
                    for j in range(NB):
                        store(e, j)
                    if e + X_SLOTS < NT:
                        load_x(e + X_SLOTS)
                if n is not None:
                    transposes("t1", n)
                if c is not None:
                    transposes("t3", c)
            for j in range(NB):
                store(NT - 1, j)
            for j in range(NB):
                sp.wait_ge(out_st[j], 16 * NT)

        @block.tensor
        def _(pe):
            def take(kind, t, i):
                m = misc_no[kind, t, i]
                if m >= 2:
                    k, t0, i0 = groups[m - 2]
                    pe.wait_ge(reader[k], 4 * t0 + i0 + 1)
                return bank(kind, t, i)

            def in_proj(kind, t, b, done):
                if b == 0:
                    wait_tile(pe, "t1", t)
                o = bank(kind, t, b) if (kind, t) == ("u", 0) else take(kind, t, b)
                c0_, s_ = (D if kind == "v" else 0) + b * P, t % 2
                for k in range(KC):
                    wh, wl = win_hi[:, k, c0_:c0_ + P], win_lo[:, k, c0_:c0_ + P]
                    pe.matmul(o[:, :], wh, x1T[:, s_, k, :], start=k == 0, stop=False)
                    pe.matmul(o[:, :], wh, x1T[:, s_, KC + k, :], start=False, stop=False)
                    mm = pe.matmul(o[:, :], wl, x1T[:, s_, k, :], start=False, stop=k == KC - 1)
                mm.then_inc(done, 1)

            def o(c, j):
                out_ = take("o", c, j)
                js = slice(j * P, (j + 1) * P)
                for k in range(KC):
                    pe.wait_ge(glo_ok, KC * c + k + 1)
                    pe.matmul(out_[:, :], g_hi[:, k, js], wo_hi[:, k, :], start=k == 0, stop=False)
                    pe.matmul(out_[:, :], g_hi[:, k, js], wo_lo[:, k, :], start=False, stop=False)
                    mm = pe.matmul(out_[:, :], g_lo[:, k, js], wo_hi[:, k, :], start=False, stop=k == KC - 1)
                mm.then_inc(o_mm, 1)

            def f1(t, j):
                i = FC * t + j
                if t == 0:
                    pe.wait_ge(w_ok, KC * (j // BQ + 1))
                if j == 0:
                    wait_tile(pe, "t3", t)
                if i >= 2:
                    pe.wait_ge(gelu_ok, i - 1)
                b, src = f1b[i % 2], x3T_of(t)
                for k in range(KC):
                    w = w1[:, k, j * P:(j + 1) * P]
                    pe.matmul(b[:, :], w, src[:, k, :], start=k == 0, stop=False)
                    mm = pe.matmul(b[:, :], w, src[:, KC + k, :], start=False, stop=k == KC - 1)
                mm.then_inc(f1_mm, 1)

            def f2_last():
                pe.wait_ge(hl_ok, FC * NT)
                for q in range(NB):
                    for j in range(FC - LAG, FC):
                        i, qs = FC * (NT - 1) + j, slice(q * P, (q + 1) * P)
                        pe.matmul(f2b[q][:, :], h_hi[:, i % H_SLOTS, qs], w2[:, j, :], start=False, stop=False)
                        mm = pe.matmul(f2b[q][:, :], h_lo[:, i % H_SLOTS, qs], w2[:, j, :], start=False, stop=j == FC - 1)
                    mm.then_inc(f2_sum, 1)

            def f2(t, j):
                i = FC * t + j
                if j == 0 and t > 0:
                    pe.wait_ge(f_ok, NB * t)
                pe.wait_ge(hl_ok, i + 1)
                if t == 0:
                    pe.wait_ge(w2_ok, j + 1)
                for q in range(NB):
                    qs = slice(q * P, (q + 1) * P)
                    pe.matmul(f2b[q][:, :], h_hi[:, i % H_SLOTS, qs], w2[:, j, :], start=j == 0, stop=False)
                    mm = pe.matmul(f2b[q][:, :], h_lo[:, i % H_SLOTS, qs], w2[:, j, :], start=False, stop=j == FC - 1)
                mm.then_inc(f2_mm, 1)

            def setup_in_proj():
                pe.wait_ge(pmx, KC + 1)
                pe.transpose(f2b[0][0:1, 0:P], wmax[:, 5:6], ident[:, :]).then_inc(pm1, 1)
                pe.wait_ge(pmx, KC + 2)
                pe.matmul(f2b[1][:, 0:1], ones[0:1, :], wrow[0:1, 0:1], start=True, stop=True).then_inc(pm1, 1)

            pe.wait_ge(const_ok, 3)
            for s in STEPS:
                fa, c, n, _ = tiles(s)
                if fa is not None:
                    for j in range(half(n)):
                        f1(fa, j)
                        if j >= LAG:
                            f2(fa, j - LAG)
                if c == 0:
                    pe.wait_ge(thr_ok, 1)
                    pe.matmul(f1b[0][:, 0:2], ones[:, :], thr_s[:, :], start=True, stop=True).then_inc(thr_mm, 1)
                    pe.wait_ge(win_l, 2 * KC)
                    for b in range(KC):
                        in_proj("u", c, b, u_mm)
                    pe.wait_ge(wo_l, KC)
                    for j in range(NB):
                        o(c, j)
                    for b in range(KC):
                        in_proj("v", n, b, v_mm)
                    continue
                left = [lambda j=j: f2(fa, j) for j in range(half(n) - LAG, half(n))] if fa is not None else 3 * [lambda: None]
                if c is not None:
                    for b in range(KC):
                        in_proj("u", c, b, u_mm)
                for f in left:
                    f()
                if c is not None:
                    for j in range(NB):
                        o(c, j)
                if n == 0:
                    setup_in_proj()
                    pe.wait_ge(win_l, KC)
                early = 2 if s != 2 else 0
                if n is not None:
                    for b in range(early):
                        in_proj("v", n, b, v_mm)
                if fa is not None:
                    for j in range(half(n), FC):
                        f1(fa, j)
                        if j >= half(n) + LAG:
                            f2(fa, j - LAG)
                late = [lambda b=b: in_proj("v", n, b, v_mm) for b in range(early, KC)] if n is not None else []
                left = [lambda j=j: f2(fa, j) for j in range(FC - LAG, FC)] if fa is not None else 3 * [lambda: None]
                if fa == NT - 1:
                    left = [f2_last]
                for f in late + left:
                    f()

        @block.vector
        def _(ve_):
            chain = [0]

            def link(ins):
                ins.then_inc(prep, 1)
                chain[0] += 1
                ve_.wait_ge(prep, chain[0])

            def stats(ln, t, j, src):
                if t > 0:
                    ve_.wait_ge(mv_ok[ln], NB * (t - 1) + j + 1)
                ve_.bn_stats(raw_stats(ln)[:, j, :], src).then_inc(bn_ok[ln], 1)

            def aggr(ln, t, j):
                ve_.wait_ge(bn_ok[ln], NB * t + j + 1)
                if t > 0:
                    ve_.wait_ge(rs_ok[ln], t)
                ve_.bn_aggr(mean_var(ln)[:, j, :], raw_stats(ln)[:, j, :]).then_inc(mv_ok[ln], 1)

            def lo(t, j):
                i = FC * t + j
                ve_.wait_ge(hh_ok, i + 1)
                ve_.scalar_tensor_tensor(out=h_lo[:, i % H_SLOTS, :], in0=gg[:, i % G_SLOTS, :],
                                         scalar=f_sc[:, j:j + 1], in1=h_hi[:, i % H_SLOTS, :],
                                         op0=ALU.mult, op1=ALU.subtract).then_inc(hl_ok, 1)

            def f_add(e, j):
                if e == NT - 1:
                    ve_.wait_ge(f2_sum, j + 1)
                elif j == 0:
                    ve_.wait_ge(f2_mm, FC * (e + 1))
                if e + 1 < NT:
                    ve_.wait_ge(x3_lo, NB * (e + 1) + j + 1)
                else:
                    ve_.wait_ge(out_st[j], 16 * e)
                ve_.tensor_tensor(hb[:, j, :], f2b[j][:, :], b2_row, ALU.add).then_inc(f_ok, 1)

            def f_stats(e, j):
                ve_.wait_ge(f_ok, NB * e + j + 1)
                stats(4, e, j, hb[:, j, :])

            def epilogue(e):
                return (spread(AT_F_ADD, .2, [lambda j=j: f_add(e, j) for j in range(NB)])
                        + spread(AT_F_STATS, .2, [lambda j=j: f_stats(e, j) for j in range(NB)])
                        + spread(AT_F_AGGR, .05, [lambda j=j: aggr(4, e, j) for j in range(NB)]))

            def ln1(n, at=AT_LN1):
                def st(j):
                    if n == 0:
                        ve_.wait_ge(x0_in[j], 16)
                    elif j == 0:
                        ve_.wait_ge(x_in[n % X_SLOTS], 16 * (n // X_SLOTS + (1 if n % X_SLOTS else 0)))
                    stats(0, n, j, xs[:, n % X_SLOTS, j, :])
                return (spread(at, .01, [lambda j=j: st(j) for j in range(NB)])
                        + spread(at + .04, .001, [lambda j=j: aggr(0, n, j) for j in range(NB)]))

            def conv_scan(c):
                def taps(b, first):
                    i = KC * c + b
                    if first:
                        ve_.wait_ge(tap1, i + 1)
                        if b == 0:
                            ve_.wait_ge(left_ok, c + 1)
                            ve_.wait_ge(right_ok, c + 1)
                        src, w, done = v[:, c % 2, b, 0:TT], par[:, CW + b:CW + b + 1], tap0
                    else:
                        ve_.wait_ge(tap0, i + 1)
                        src, w, done = v[:, c % 2, b, 2:TT + 2], par[:, CW + 8 + b:CW + 9 + b], tap2
                    dst = vl[:, i % 2, :]
                    ve_.scalar_tensor_tensor(out=dst, in0=src, scalar=w, in1=dst,
                                             op0=ALU.mult, op1=ALU.add).then_inc(done, 1)

                def scan(b):
                    i = KC * c + b
                    ve_.wait_ge(tap2, i + 1)
                    if i >= 2:
                        ve_.wait_ge(y_ok, i - 1)
                        ve_.wait_ge(carry_ok, i - 1)
                    if c > 0:
                        ve_.wait_ge(carry_ok, i - KC + 1)
                    ve_.tensor_tensor_scan(out=ss[:, i % 2, :], data0=a_par[:, b:b + 1].to_broadcast([P, TT]),
                                           data1=vl[:, i % 2, :],
                                           initial=carry[:, b:b + 1] if c > 0 else 0.0,
                                           op0=ALU.mult, op1=ALU.add).then_inc(scan_ok, 1)

                def y(b):
                    i = KC * c + b
                    ve_.wait_ge(scan_ok, i + 1)
                    ve_.wait_ge(dv_ok, i + 1)
                    dst = yb[:, b, :]
                    ve_.scalar_tensor_tensor(out=dst, in0=ss[:, i % 2, :], scalar=cb_par[:, b:b + 1], in1=dst,
                                             op0=ALU.mult, op1=ALU.add).then_inc(y_ok, 1)

                items = []
                for b, at in zip(range(0, KC, 2), AT_PAIR):
                    items += spread(at, .2, [lambda b=b: taps(b, True), lambda b=b: taps(b + 1, True),
                                             lambda b=b: taps(b, False), lambda b=b: taps(b + 1, False)])
                    items += spread(at + .9, .4, [lambda b=b: scan(b), lambda b=b: scan(b + 1)])
                    items += spread(at + 1.8, .2, [lambda b=b: y(b), lambda b=b: y(b + 1)])
                return items

            def gate(c, b):
                i = KC * c + b
                ve_.wait_ge(sy_ok, i + 1)
                ve_.wait_ge(u_mm, i + 1)
                dst = yb[:, b, :]
                ve_.scalar_tensor_tensor(out=dst, in0=bank("u", c, b)[:, :], scalar=bu_sig[:, b:b + 1], in1=dst,
                                         op0=ALU.add, op1=ALU.mult).then_inc(g_ok, 1)

            def gate_lo(c, b):
                ve_.wait_ge(ghi_ok, KC * c + b + 1)
                ve_.tensor_tensor(g_lo[:, b, :], yb[:, b, :], g_hi[:, b, :].bitcast(F32),
                                  ALU.subtract).then_inc(glo_ok, 1)

            def t_lo(kind, t, j):
                src, ok, done = (xn[:, :], x1_hi, x1_lo) if kind == "t1" else (hb[:, j, :], x3_hi, x3_lo)
                r = block_no[kind, t, j] % T_SLOTS
                ve_.wait_ge(ok, NB * t + j + 1)
                ve_.scalar_tensor_tensor(out=tp[:, r, 1, :], in0=src, scalar=ACT_SCALE, in1=tp[:, r, 0, :],
                                         op0=ALU.mult, op1=ALU.subtract).then_inc(done, 1)

            def h_add(c, j):
                ve_.wait_ge(o_mm, NB * c + j + 1)
                ve_.wait_ge(resb_ok, NB * c + j + 1)
                ve_.scalar_tensor_tensor(out=hb[:, j, :], in0=bank("o", c, j)[:, :], scalar=inv_sig[:, 0:1],
                                         in1=hb[:, j, :], op0=ALU.mult, op1=ALU.add).then_inc(h_ok, 1)

            def h_stats(c, j):
                ve_.wait_ge(h_ok, NB * c + j + 1)
                stats(1, c, j, hb[:, j, :])

            def norms(c):
                xsl = xs[:, c % X_SLOTS]

                def a1(j):
                    if j == 0:
                        ve_.wait_ge(rs_ok[1], c + 1)
                    ve_.scalar_tensor_tensor(out=hb[:, j, :], in0=hb[:, j, :], scalar=mean_var(1)[:, j, 0:1],
                                             in1=lnw_row, op0=ALU.subtract, op1=ALU.mult).then_inc(a1_ok, 1)

                def a2(j):
                    ve_.wait_ge(a1_ok, NB * c + j + 1)
                    ve_.scalar_tensor_tensor(out=hb[:, j, :], in0=hb[:, j, :], scalar=rsc[:, 0, j:j + 1],
                                             in1=lnb_row, op0=ALU.mult, op1=ALU.add).then_inc(a2_ok, 1)

                def b_stats(j):
                    ve_.wait_ge(a2_ok, NB * c + j + 1)
                    stats(2, c, j, hb[:, j, :])

                def x1(j):
                    if j == 0:
                        ve_.wait_ge(rs_ok[2], c + 1)
                    ve_.scalar_tensor_tensor(out=xsl[:, j, :], in0=hb[:, j, :], scalar=rsc[:, 1, j:j + 1],
                                             in1=xsl[:, j, :], op0=ALU.mult, op1=ALU.add).then_inc(x1_ok, 1)

                def c_stats(j):
                    ve_.wait_ge(x1_ok, NB * c + j + 1)
                    stats(3, c, j, xsl[:, j, :])

                def n3(j):
                    if j == 0:
                        ve_.wait_ge(rs_ok[3], c + 1)
                    ve_.tensor_scalar(hb[:, j, :], xsl[:, j, :], mean_var(3)[:, j, 0:1], rsc[:, 2, j:j + 1],
                                      ALU.subtract, ALU.mult).then_inc(n3_ok, 1)

                kinds = [a1, a2, b_stats, lambda j: aggr(2, c, j), x1, c_stats, lambda j: aggr(3, c, j), n3]
                return spread(AT_NORMS if c < NT - 2 else AT_NORMS_END, .25, [lambda f=f, j=j: f(j) for f in kinds for j in range(NB)])

            def setup_in_proj():
                for k in range(KC):
                    ve_.wait_ge(win_in[k], 16)
                    ve_.tensor_reduce(wmax[:, k:k + 1], wf[:, k, :], AX.X, ALU.max,
                                      apply_absolute_value=True).then_inc(pmx, 1)
                    if k:
                        t_lo("t1", 0, k - 1)
                ve_.wait_ge(pmx, KC)
                link(ve_.tensor_reduce(wmax[:, 4:5], wmax[:, 0:KC], AX.X, ALU.max))
                ve_.tensor_scalar(wmax[:, 5:6].bitcast(U32), wmax[:, 4:5].bitcast(U32), 0x7F800000, None,
                                  ALU.bitwise_and).then_inc(pmx, 1)
                t_lo("t1", 0, NB - 1)
                ve_.wait_ge(pm1, 1)
                ve_.tensor_reduce(wrow[0:1, 0:1], f2b[0][0:1, 0:P], AX.X, ALU.max).then_inc(pmx, 1)
                ve_.wait_ge(pm1, 2)
                ve_.tensor_scalar(wmax[:, 6:7], f2b[1][:, 0:1], 2.0 ** -100, 2.0 ** -13,
                                  ALU.max, ALU.mult).then_inc(pmx, 1)
                ve_.wait_ge(pmx, KC + 3)
                link(ve_.reciprocal(wmax[:, 7:8], wmax[:, 6:7]))
                link(ve_.tensor_scalar(inv_sig[:, :], wmax[:, 6:7], 1.0 / ACT_SCALE, None, ALU.mult))
                link(ve_.tensor_scalar(sig[:, :], wmax[:, 7:8], ACT_SCALE, None, ALU.mult))

            def setup_split(part):
                for i in part:
                    k, hs = i % KC, (D if i < KC else 0)
                    ve_.wait_ge(win_h, i + 1)
                    ve_.scalar_tensor_tensor(out=win_lo[:, k, hs:hs + D], in0=wf[:, k, hs:hs + D],
                                             scalar=wmax[:, 7:8], in1=win_hi[:, k, hs:hs + D],
                                             op0=ALU.mult, op1=ALU.subtract).then_inc(win_l, 1)

            def setup_params():
                ve_.wait_ge(par_in, 16)
                link(ve_.tensor_scalar(bu_sig[:, :], par[:, BIN:BIN + KC], sig[:, 0:1], None, ALU.mult))
                link(ve_.tensor_tensor(cb_par[:, :], par[:, SC:SC + KC], par[:, SB:SB + KC], ALU.mult))
                ve_.wait_ge(tanh_ok, 1)
                ve_.tensor_scalar(a_par[:, :], a_par[:, :], 1.0, 0.5, ALU.add, ALU.mult).then_inc(a_ok, 1)
                ve_.wait_ge(a_ok, 1)
                link(ve_.tensor_scalar(f_inv[:, :].bitcast(U32), par[:, B1:B1 + FC].bitcast(U32), 0x7FFFFFFF, None,
                                       ALU.bitwise_and))
                link(ve_.tensor_scalar(f_sc[:, :], f_inv[:, :], 512.0, None, ALU.add))
                link(ve_.tensor_scalar(f_inv[:, :].bitcast(U32), f_sc[:, :].bitcast(U32), 0x7F800000, None,
                                       ALU.bitwise_and))
                link(ve_.tensor_scalar(f_inv[:, :], f_inv[:, :], 2.0 ** -14, None, ALU.mult))
                link(ve_.reciprocal(f_sc[:, :], f_inv[:, :]))

            def setup_out_proj(k):
                ve_.wait_ge(wo_h, k + 1)
                ve_.tensor_tensor(wo_lo[:, k, :], yb[:, k, :], wo_hi[:, k, :].bitcast(F32),
                                  ALU.subtract).then_inc(wo_l, 1)

            def setup_thresholds():
                ve_.wait_ge(abs_ok[0], NCH // 2)
                ve_.wait_ge(abs_ok[1], NCH // 2)
                link(ve_.tensor_reduce(thr_s[:, 0:1], asum[:, 0:NCH // 2], AX.X, ALU.add))
                ve_.tensor_reduce(thr_s[:, 1:2], asum[:, NCH // 2:NCH], AX.X, ALU.add).then_inc(thr_ok, 1)
                ve_.wait_ge(thr_mm, 1)
                link(ve_.tensor_scalar(thr[:, 0:2], f1b[0][:, 0:2], 1.0 / (D * FF), 1e-8, ALU.mult, ALU.max))
                link(ve_.tensor_scalar(thr[:, 0:2], thr[:, 0:2], 0.5, None, ALU.mult))
                ve_.tensor_scalar(thr[:, 2:4], thr[:, 0:2], -1.0, None, ALU.mult).then_inc(thr_ok, 1)
                ve_.wait_ge(thr_ok, 2)

            def abs_sum(i):
                slot, loaded = sum_slot(i)
                ve_.wait_ge(chunk_in[slot], loaded)
                ve_.tensor_reduce(asum[:, i:i + 1], wch[:, slot, :], AX.X, ALU.add,
                                  apply_absolute_value=True).then_inc(abs_ok[1], 1)

            def ternary(i):
                m, (slot, _) = i // (NCH // 2), conv_slot(i)
                if i not in W_GPSIMD:
                    first_summand(ve_, i, td_ok)
                ve_.wait_ge(tp_ok if i in W_GPSIMD else td_ok, first_no(i))
                ve_.scalar_tensor_tensor(out=chunk_dst(i), in0=wch[:, slot, :], scalar=thr[:, m:m + 1],
                                         in1=chunk_dst(i), op0=ALU.is_gt, op1=ALU.add).then_inc(w_ok, 1)

            run(ln1(0))
            setup_in_proj()
            for s in STEPS:
                fa, c, n, e = tiles(s)
                items = []
                if e is not None:
                    items += epilogue(e)
                if n is not None and s > 2:
                    items += ln1(n)
                if c is not None:
                    items += conv_scan(c)
                if s == 1:
                    for b, at in zip(range(0, KC, 2), AT_PAIR):
                        items += spread(at + 2.1, .1, [lambda b=b: gate(c, b), lambda b=b: gate(c, b + 1),
                                                       lambda b=b: gate_lo(c, b), lambda b=b: gate_lo(c, b + 1)])
                    items += ln1(n, AT_PAIR[0] + .85)
                    items += [(at, lambda j=j: t_lo("t1", n, j)) for j, at in enumerate(AT_T_LO)]
                    items += [(AT_W_PAIRS[i], lambda i=i: ternary(i)) for i in range(W_PAIRS)]
                if fa is not None:
                    items += spread(1.2, 1, [lambda j=j: lo(fa, j) for j in range(half(n))])
                if s == 2:
                    items += [(at_w(i) + 1.2, lambda i=i: ternary(i)) for i in range(W_NORMS, NCH - NB)]
                run(items)
                front = n is not None and n > 3
                if c is not None and c > 0:
                    gate(c, 0)
                    gate(c, 1)
                if front:
                    t_lo("t1", n, 0)
                if c is not None and c > 0:
                    gate_lo(c, 0)
                    gate(c, 2)
                    gate_lo(c, 1)
                if front:
                    t_lo("t1", n, 1)
                if c is not None and c > 0:
                    gate(c, 3)
                    gate_lo(c, 2)
                    gate_lo(c, 3)
                if front:
                    t_lo("t1", n, 2)
                    t_lo("t1", n, 3)
                if s == -1:
                    setup_split(range(KC))
                    run(ln1(1))
                    setup_split(range(KC, 2 * KC))
                    for j, part in enumerate(((), (1, 3), (5, 7), (9, 11))):
                        for i in part:
                            abs_sum(i)
                        t_lo("t1", 1, j)
                    setup_params()
                    abs_sum(13)
                    abs_sum(15)
                if s == 0:
                    for k in range(KC):
                        setup_out_proj(k)
                    for i in range(NCH // 2 + 1, NCH, 2):
                        abs_sum(i)
                    setup_thresholds()
                items = []
                if c is not None:
                    for j in range(NB):
                        if s in (1, 2):
                            ternary((W_PAIRS if s == 1 else NCH - NB) + j)
                        h_add(c, j)
                        if j:
                            h_stats(c, j - 1)
                            if j > 1:
                                aggr(1, c, j - 2)
                    h_stats(c, NB - 1)
                    aggr(1, c, NB - 2)
                    aggr(1, c, NB - 1)
                    items = norms(c)
                if s == 2:
                    items += ln1(n, 9.9)
                    items += [(at, lambda j=j: t_lo("t1", n, j)) for j, at in enumerate(AT_T_LO_2)]
                if s == 1:
                    items += [(at_w(i), lambda i=i: ternary(i)) for i in range(W_OUT, W_NORMS)]
                if fa is not None:
                    items += spread(half(n) + (.2 if s == 2 or n is None else 1.2), 1,
                                    [lambda j=j: lo(fa, j) for j in range(half(n), FC)])
                if c is not None:
                    items += [(at, lambda j=j: t_lo("t3", c, j)) for j, at in enumerate(AT_T3_LO if n is not None else AT_T3_LO_END)]
                run(items)
            e = NT - 1
            for j in range(NB + 1):
                if j < NB:
                    f_add(e, j)
                    f_stats(e, j)
                    aggr(4, e, j)
                if j:
                    ve_.wait_ge(fn_ok, NB * e + j)
                    ve_.tensor_tensor(hb[:, j - 1, :], hb[:, j - 1, :], xs[:, e % X_SLOTS, j - 1, :],
                                      ALU.add).then_inc(fin_last, 1)

        @block.scalar
        def _(act):
            def gelu(t, j):
                i = FC * t + j
                act.wait_ge(f1_mm, i + 1)
                if i >= G_SLOTS:
                    act.wait_ge(hl_ok, i - G_SLOTS + 1)
                act.activation(gg[:, i % G_SLOTS, :], f1b[i % 2][:, :], ACT.Gelu,
                               bias=par[:, B1 + j:B1 + j + 1], scale=1.0 / ACT_SCALE).then_inc(gelu_ok, 1)

            def hi(t, j):
                i = FC * t + j
                act.wait_ge(gelu_ok, i + 1)
                if i >= H_SLOTS:
                    act.wait_ge(f2_mm, i - H_SLOTS + 1)
                else:
                    act.wait_ge(abs_ok[0], NCH // 2)
                act.activation(h_hi[:, i % H_SLOTS, :], gg[:, i % G_SLOTS, :], ACT.Copy,
                               scale=f_sc[:, j:j + 1]).then_inc(hh_ok, 1)

            def ffn(t, js):
                return (spread(js[0], 1, [lambda j=j: gelu(t, j) for j in js])
                        + spread(js[0] + 1.1, 1, [lambda j=j: hi(t, j) for j in js]))

            def ffn_norm(e, j):
                if j == 0:
                    act.wait_ge(rs_ok[4], e + 1)
                act.activation(hb[:, j, :], hb[:, j, :], ACT.Identity, bias=nm4[:, j:j + 1],
                               scale=rs4[:, j:j + 1]).then_inc(fn_ok, 1)

            def centre_tap(c, b):
                i = KC * c + b
                act.wait_ge(v_ok, i + 1)
                if i >= 2:
                    act.wait_ge(scan_ok, i - 1)
                    act.wait_ge(dv_ok, i - 1)
                act.activation(vl[:, i % 2, :], v[:, c % 2, b, 1:TT + 1], ACT.Identity,
                               bias=par[:, CB + b:CB + b + 1], scale=par[:, CW + 4 + b:CW + 5 + b]).then_inc(tap1, 1)

            def d_conv(c, b):
                i = KC * c + b
                act.wait_ge(tap2, i + 1)
                if c > 0:
                    act.wait_ge(glo_ok, i - KC + 1)
                elif b == 0:
                    act.wait_ge(wo_l, KC)
                act.activation(yb[:, b, :], vl[:, i % 2, :], ACT.Copy,
                               scale=par[:, SD + b:SD + b + 1]).then_inc(dv_ok, 1)

            def residual(c, j):
                if c > 0:
                    act.wait_ge(x3_lo, NB * (c - 1) + j + 1)
                if c > 1:
                    act.wait_ge(out_st[j], 16 * (c - 1))
                act.activation(hb[:, j, :], xs[:, c % X_SLOTS, j, :], ACT.Identity, bias=nm1[:, c % 4, j:j + 1],
                               scale=rs1[:, c % 4, j:j + 1]).then_inc(res_ok, 1)

            def silu_y(c, b):
                act.wait_ge(y_ok, KC * c + b + 1)
                act.activation(yb[:, b, :], yb[:, b, :], ACT.Silu).then_inc(sy_ok, 1)

            def gate_hi(c, b):
                act.wait_ge(g_ok, KC * c + b + 1)
                if b == 0 and c > 0:
                    act.wait_ge(o_mm, NB * c)
                act.activation(g_hi[:, b, :], yb[:, b, :], ACT.Copy).then_inc(ghi_ok, 1)

            def norm_x(n, j):
                i = NB * n + j
                if j == 0:
                    act.wait_ge(rs_ok[0], n + 1)
                if i > 0:
                    act.wait_ge(x1_lo, i)
                act.activation(xn[:, :], xs[:, n % X_SLOTS, j, :], ACT.Identity, bias=nm1[:, n % 4, j:j + 1],
                               scale=rs1[:, n % 4, j:j + 1]).then_inc(xn_ok, 1)

            def t_hi(kind, t, j):
                src, ok, done = (xn[:, :], xn_ok, x1_hi) if kind == "t1" else (hb[:, j, :], n3_ok, x3_hi)
                m = block_no[kind, t, j]
                act.wait_ge(ok, NB * t + j + 1)
                if m >= T_SLOTS:
                    wait_transposed(act, m - T_SLOTS)
                act.activation(tp[:, m % T_SLOTS, 0, :], src, ACT.Copy, scale=ACT_SCALE).then_inc(done, 1)

            def front(n, j):
                norm_x(n, j)
                t_hi("t1", n, j)

            def silu_v(n, b):
                act.wait_ge(v_mm, KC * n + b + 1)
                if n > 1 and b == 0:
                    act.wait_ge(tap2, KC * (n - 1))
                if n == 0 and b == 0:
                    act.wait_ge(win_l, 2 * KC)
                if n > 0 and b == 0:
                    act.wait_ge(left_ok, n)
                    if n > 1:
                        act.wait_ge(right_ok, n - 1)
                act.activation(v[:, n % 2, b, 1:TT + 1], bank("v", n, b)[:, :], ACT.Silu,
                               bias=par[:, BIN + KC + b:BIN + KC + b + 1], scale=inv_sig[:, 0:1]).then_inc(v_ok, 1)

            def abs_sum(i):
                slot, loaded = sum_slot(i)
                act.wait_ge(chunk_in[slot], loaded)
                n = i // 2
                if n >= H_SLOTS:
                    act.wait_ge(abs_ok[0], n - H_SLOTS + 1)
                act.activation(h_hi[:, n % H_SLOTS, :], wch[:, slot, :], ACT.Abs,
                               accum_out=asum[:, i:i + 1]).then_inc(abs_ok[0], 1)

            def scale_w2(j):
                act.wait_ge(w_ok, NCH // 2 + j + 1)
                act.activation(w2[:, j, :], w2[:, j, :], ACT.Copy, scale=f_inv[:, j:j + 1]).then_inc(w2_ok, 1)

            act.wait_ge(par_in, 16)
            act.activation(a_par[:, :], par[:, LA:LA + KC], ACT.Tanh, scale=0.5).then_inc(tanh_ok, 1)
            for s in STEPS:
                fa, c, n, e = tiles(s)
                items = []
                if e is not None:
                    items += [(at, lambda j=j: ffn_norm(e, j)) for j, at in enumerate(AT_F_NORM)]
                if c is not None:
                    for b, at in zip(range(0, KC, 2), AT_PAIR):
                        items += spread(at - .3, .15, [lambda b=b: centre_tap(c, b), lambda b=b: centre_tap(c, b + 1)])
                        items += spread(at + 1.2, .4, [lambda b=b: d_conv(c, b), lambda b=b: d_conv(c, b + 1)])
                if fa is not None:
                    items += ffn(fa, range(half(n)))
                if s == 1:
                    for b, at in zip(range(0, KC, 2), AT_PAIR):
                        items += spread(at + 2.05, .1, [lambda b=b: silu_y(c, b), lambda b=b: silu_y(c, b + 1),
                                                        lambda b=b: gate_hi(c, b), lambda b=b: gate_hi(c, b + 1)])
                    items += spread(AT_PAIR[0] + .9, .01, [lambda j=j: residual(c, j) for j in range(NB)])
                    items += [(at, lambda j=j: front(n, j)) for j, at in enumerate(AT_FRONT)]
                    items += [(AT_PAIR[1] + at, lambda b=b: silu_v(n, b)) for b, at in enumerate((3.0, 3.01, 3.02, 3.03))]
                    run(items)
                    items = [lambda j=j: t_hi("t3", c, j) for j in range(NB)]
                    for f in items:
                        f()
                    continue
                if s == 2:
                    items += [(at_w(i) + 2.1, lambda i=i: scale_w2(i - NCH // 2)) for i in range(NCH // 2, NCH - NB)]
                run(items)
                if c is not None and c > 0:
                    for b in range(KC):
                        silu_y(c, b)
                works = [[], [], [], []]
                if c is not None and c > 0:
                    works = [[lambda: gate_hi(c, 0), lambda: gate_hi(c, 1)],
                             [lambda: gate_hi(c, 2), lambda: residual(c, 0), lambda: gate_hi(c, 3)],
                             [lambda: residual(c, 1), lambda: residual(c, 2)], [lambda: residual(c, 3)]]
                if s == 2:
                    works = [[], [], [], sum(works, [])]
                for j in range(NB):
                    if n is not None and n not in (1, 3):
                        front(n, j)
                    for work in works[j]:
                        work()
                if s == -1:
                    act.wait_ge(prep, 2)
                    for i in range(2 * KC):
                        k, hs = i % KC, (D if i < KC else 0)
                        act.activation(win_hi[:, k, hs:hs + D], wf[:, k, hs:hs + D], ACT.Copy,
                                       scale=wmax[:, 7:8]).then_inc(win_h, 1)
                if s == 0:
                    act.wait_ge(wout_in, 16)
                    for k in range(KC):
                        act.activation(wo_hi[:, k, :], yb[:, k, :], ACT.Copy).then_inc(wo_h, 1)
                for i in ABS_AFTER_V.get((n, -1), ()):
                    abs_sum(2 * i)
                items = ffn(fa, range(half(n), FC)) if fa is not None else []
                if s == 2:
                    items += [(at, lambda j=j: front(n, j)) for j, at in enumerate(AT_FRONT_2)]
                    items += [(at, lambda j=j: scale_w2(j)) for j, at in enumerate(AT_SCALE_LAST, FC - NB)]
                if n is not None:
                    for b, at in enumerate(AT_V if s != 2 else AT_V_2):
                        if s == -1:
                            items.append((at, lambda j=b: front(1, j)))
                        items.append((at, lambda b=b: silu_v(n, b)))
                        items += [(at, lambda i=i: abs_sum(2 * i)) for i in ABS_AFTER_V.get((n, b), ())]
                if c is not None:
                    items += [(at, lambda j=j: t_hi("t3", c, j))
                              for j, at in enumerate(AT_T3_HI if n is not None else AT_T3_HI_END)]
                run(items)
            for j in range(NB):
                act.wait_ge(rs_ok[4], NT + j)
                ffn_norm(NT - 1, j)

        @block.gpsimd
        def _(pool):
            chain = [0]

            def link(ins):
                ins.then_inc(pool_ok, 1)
                chain[0] += 1
                pool.wait_ge(pool_ok, chain[0])

            def rstd(ln, t, dst, last, js=slice(0, NB)):
                pool.wait_ge(mv_ok[ln], NB * t + js.stop)
                link(pool.tensor_scalar(ve[:, ln, js], mean_var(ln)[:, js, 1], EPS, None, ALU.add))
                ins = pool.tensor_tensor(dst, ve[:, ln, js], mhalf[:, js], ALU.pow)
                if last:
                    ins.then_inc(rs_ok[ln], 1)
                else:
                    link(ins)

            def rstd_x(n):
                if n > 3:
                    pool.wait_ge(res_ok, NB * (n - 3))
                rstd(0, n, rs1[:, n % 4, :], False)
                link(pool.tensor_tensor(tmp4[:, 0, :], mean_var(0)[:, :, 0], rs1[:, n % 4, :], ALU.mult))
                pool.tensor_scalar(nm1[:, n % 4, :], tmp4[:, 0, :], -1.0, None, ALU.mult).then_inc(rs_ok[0], 1)

            def rstd_b(c):
                rstd(2, c, rsc[:, 1, :], False)
                pool.tensor_tensor(c0[:, c % 4, :], mean_var(2)[:, :, 0], rsc[:, 1, :], ALU.mult).then_inc(rs_ok[2], 1)

            def rstd_f(e, js=slice(0, NB)):
                if e > 0:
                    pool.wait_ge(fn_ok, NB * e)
                rstd(4, e, rs4[:, js], False, js)
                link(pool.tensor_tensor(tmp4[:, 1, js], mean_var(4)[:, js, 0], rs4[:, js], ALU.mult))
                link(pool.tensor_tensor(tmp4[:, 2, js], tmp4[:, 1, js], c0[:, e % 4, js], ALU.add))
                pool.tensor_scalar(nm4[:, js], tmp4[:, 2, js], -1.0, None, ALU.mult).then_inc(rs_ok[4], 1)

            def finish(e, j):
                pool.wait_ge(fn_ok, NB * e + j + 1)
                pool.tensor_tensor(hb[:, j, :], hb[:, j, :], xs[:, e % X_SLOTS, j, :], ALU.add).then_inc(fin_ok, 1)

            def keep_state(c, b):
                i = KC * c + b
                pool.wait_ge(scan_ok, i + 1)
                pool.tensor_copy(carry[:, b:b + 1], ss[:, i % 2, TT - 1:TT]).then_inc(carry_ok, 1)

            def add_bias(c, j):
                pool.wait_ge(res_ok, NB * c + j + 1)
                pool.tensor_tensor(hb[:, j, :], hb[:, j, :], ob_row, ALU.add).then_inc(resb_ok, 1)

            def edges(n):
                if n < NT:
                    pool.wait_ge(v_ok, KC * (n + 1))
                if n == 0:
                    pool.memset(v[:, 0, :, 0:1], 0.0).then_inc(left_ok, 1)
                    return
                if n < NT:
                    if n > 1:
                        pool.wait_ge(tap2, KC * (n - 1))
                    pool.tensor_copy(v[:, n % 2, :, 0:1], v[:, (n - 1) % 2, :, TT:TT + 1]).then_inc(left_ok, 1)
                    pool.tensor_copy(v[:, (n - 1) % 2, :, TT + 1:TT + 2], v[:, n % 2, :, 1:2]).then_inc(right_ok, 1)
                else:
                    pool.memset(v[:, (n - 1) % 2, :, TT + 1:TT + 2], 0.0).then_inc(right_ok, 1)

            pool.memset(ident[:, :], 0.0).then_inc(const_ok, 1)
            pool.memset(ones[:, :], 1.0).then_inc(const_ok, 1)
            pool.wait_ge(const_ok, 2)
            pool.affine_select(out=ident[:, :], in_=ident[:, :], compare_op=ALU.not_equal, fill=1.0, base=0,
                               pattern=[[-1, P]], channel_multiplier=1).then_inc(const_ok, 1)
            link(pool.memset(mhalf[:, :], -0.5))
            for s in STEPS:
                fa, c, n, e = tiles(s)
                if e is not None:
                    rstd_f(e)
                    for j in range(NB):
                        finish(e, j)
                items = []
                if c is not None:
                    for b, at in zip(range(0, KC, 2), AT_PAIR):
                        items += spread(at + 1.0, .4, [lambda b=b: keep_state(c, b), lambda b=b: keep_state(c, b + 1)])
                if s == 1:
                    items.append((AT_PAIR[0] + 1.0, lambda: rstd_x(n)))
                    items.append((at_w(0) - .01, lambda: pool.wait_ge(thr_ok, 2)))
                    items += [(at_w(i), lambda i=i: first_summand(pool, i, tp_ok)) for i in range(W_PAIRS) if i in W_GPSIMD]
                if s == 2:
                    items += [(at_w(i), lambda i=i: first_summand(pool, i, tp_ok)) for i in range(W_NORMS, NCH) if i in W_GPSIMD]
                run(items)
                if n is not None and s > 2:
                    rstd_x(n)
                if s < 0:
                    rstd_x(0)
                    rstd_x(1)
                if c == 0:
                    pool.wait_ge(row_in, 16)
                    for j in range(NB):
                        add_bias(c, j)
                    rstd(1, c, rsc[:, 0, :], True)
                    first_summand(pool, 13, tp_ok)
                    rstd_b(c)
                    edges(n)
                    rstd(3, c, rsc[:, 2, :], True)
                    continue
                if c is not None:
                    for j in range(NB):
                        add_bias(c, j)
                if c is not None:
                    rstd(1, c, rsc[:, 0, :], True)
                    if s == 2:
                        rstd_x(n)
                    rstd_b(c)
                    rstd(3, c, rsc[:, 2, :], True)
                if n is not None:
                    edges(n)
                if s == NT - 1:
                    edges(NT)
            for j in range(NB):
                rstd_f(NT - 1, slice(j, j + 1))


def kernel(**inputs):
    import numpy as np
    import concourse.bacc as bacc
    from concourse.bass_utils import run_bass_kernel_spmd

    def get(name):
        return np.asarray(inputs[name])

    x = get("L0_attn_x")
    cols = [get("L0_attn_in_proj_b").reshape(-1, P)]
    cols += [get("L0_attn_conv_w")[:, 0, k].reshape(-1, P) for k in range(3)]
    cols += [get("L0_attn_" + n).reshape(-1, P) for n in ("conv_b", "logit_a", "ssm_b", "ssm_c", "ssm_d")]
    cols += [get("L0_ffn_b1").reshape(-1, P)]
    arrays = {
        "x_dram": x.reshape(-1, D),
        "w_in_dram": get("L0_attn_in_proj_w"),
        "w_out_dram": get("L0_attn_out_proj_w"),
        "w1t_dram": get("L0_ffn_W1").T,
        "w2t_dram": get("L0_ffn_W2").T,
        "params_dram": np.concatenate(cols, axis=0).T,
        "rows_dram": np.stack([get("L0_attn_out_proj_b"), get("L0_attn_ln_w"), get("L0_attn_ln_b"), get("L0_ffn_b2")]),
    }
    arrays = {n: np.ascontiguousarray(a) for n, a in arrays.items()}
    nc = bacc.Bacc("TRN2", target_bir_lowering=False, num_devices=1)
    args = [nc.dram_tensor(n, a.shape, mybir.dt.from_np(a.dtype), kind="ExternalInput").ap() for n, a in arrays.items()]
    out = nc.dram_tensor("out_dram", arrays["x_dram"].shape, F32, kind="ExternalOutput").ap()
    build(nc, *args, out)
    r = run_bass_kernel_spmd(nc, [arrays], core_ids=[0])
    return r.results[0]["out_dram"].reshape(x.shape)
```
